# Optimizing a Trainium2 kernel written in Bass

```python
import numpy as np
import jax
import jax.numpy as jnp

def _softmax(x, axis=-1):
    return jax.nn.softmax(x, axis=axis)

def _gelu(x):
    return jax.nn.gelu(x, approximate=True)

def _silu(x):
    return jax.nn.silu(x)

def _sigmoid(x):
    return jax.nn.sigmoid(x)

def _layernorm(x, axis=-1, eps=1e-05):
    m = jnp.mean(x, axis=axis, keepdims=True)
    v = jnp.var(x, axis=axis, keepdims=True)
    return (x - m) / jnp.sqrt(v + eps)

def _scatter_add(tgt, idx, src, axis=0):
    return tgt.at[idx].add(src)

def _segment_sum(src, seg, n):
    return jax.ops.segment_sum(src, seg, n)
kernel_name = 'mk_flamingo_gated_d2_seqx_r4_599015'

def setup_inputs(seed: int=0):
    np.random.seed(seed)
    _w = jnp.asarray

    def _rec_inputs():
        import jax
        import jax.numpy as jnp
        _rk = jax.random.key(seed)
        x = -0.0002928 + 1 * jax.random.normal(jax.random.fold_in(_rk, 1), (8, 256, 256), jnp.float32)
        _lenS = 256 - jax.random.randint(jax.random.fold_in(_rk, 7), (8,), 0, max(1, 256 // 4) + 1, jnp.int32)
        _lenS2 = 256 - jax.random.randint(jax.random.fold_in(_rk, 8), (8,), 0, max(1, 256 // 4) + 1, jnp.int32)
        _ctx_1024P = jax.random.normal(jax.random.fold_in(_rk, 11), (8, 16, 256), jnp.float32)
        _ctx_1024c = jax.random.dirichlet(jax.random.fold_in(_rk, 511), 0.3 * jnp.ones((16,), jnp.float32), (8, 256))
        _ctx_1024t = jnp.einsum('bsk,bkd->bsd', _ctx_1024c, _ctx_1024P)
        _ctx_1024t = _ctx_1024t * jax.lax.rsqrt(jnp.mean(jnp.square(_ctx_1024t)) + 1e-12) * 0.953939
        ctx_1024 = -1.39393e-06 + 0.999914 * (_ctx_1024t + 0.3 * jax.random.normal(jax.random.fold_in(_rk, 611), (8, 256, 256), jnp.float32))
        _validS = jnp.arange(256)[None, :] < _lenS[:, None]
        _validS2 = jnp.arange(256)[None, :] < _lenS2[:, None]
        _causal = jnp.tril(jnp.ones((256, 256), dtype=bool))
        mask_BxSxS2_if1 = jnp.where(jnp.ones((8, 256, 256), dtype=bool), 1, 0).astype(jnp.int32)
        _g = jax.random.normal(jax.random.fold_in(_rk, 9001), (2, 2), jnp.float32)
        _g = jnp.sign(_g) * jnp.maximum(jnp.abs(_g), 1.0) + (_g == 0) * 1.0
        g_xattn = _g[0]
        g_ffn = _g[1]
        return (x, ctx_1024, mask_BxSxS2_if1, g_xattn, g_ffn)
    x, ctx_1024, mask_BxSxS2_if1, g_xattn, g_ffn = _rec_inputs()

    def _L0_xattn_setup():
        import jax, jax.numpy as jnp
        import numpy as np
        EMBED_DIM = 256
        NUM_HEADS = 16
        HEAD_DIM = EMBED_DIM // NUM_HEADS
        B, T_Q, T_K = (2, 512, 512)
        key = jax.random.key(seed)
        ks = jax.random.split(key, 11)
        s = 1.0 / np.sqrt(EMBED_DIM)
        return {'query': jax.random.normal(ks[0], (B, T_Q, EMBED_DIM), jnp.float32), 'key': jax.random.normal(ks[1], (B, T_K, EMBED_DIM), jnp.float32), 'value': jax.random.normal(ks[2], (B, T_K, EMBED_DIM), jnp.float32), 'Wq': jax.random.normal(ks[3], (EMBED_DIM, EMBED_DIM), jnp.float32) * s, 'bq': jnp.zeros((EMBED_DIM,), jnp.float32), 'Wk': jax.random.normal(ks[4], (EMBED_DIM, EMBED_DIM), jnp.float32) * s, 'bk': jnp.zeros((EMBED_DIM,), jnp.float32), 'Wv': jax.random.normal(ks[5], (EMBED_DIM, EMBED_DIM), jnp.float32) * s, 'bv': jnp.zeros((EMBED_DIM,), jnp.float32), 'Wo': jax.random.normal(ks[6], (EMBED_DIM, EMBED_DIM), jnp.float32) * s, 'bo': jnp.zeros((EMBED_DIM,), jnp.float32)}
    _L0_xattn_all = _L0_xattn_setup()
    _L0_xattn_in = {k: v for k, v in _L0_xattn_all.items() if k in ('Wq', 'bq', 'Wk', 'bk', 'Wv', 'bv', 'Wo', 'bo')}
    del _L0_xattn_all

    def _L0_ffn_setup():
        import jax, jax.numpy as jnp
        import numpy as np
        D_MODEL, D_FF, N_EXPERTS, TOP_K = (256, 1024, 8, 2)
        key = jax.random.key(seed)
        k0, k1, k2, k3 = jax.random.split(key, 4)
        x = jax.random.normal(k0, (2, 512, D_MODEL), dtype=jnp.float32)
        gate_w = jax.random.normal(k1, (D_MODEL, N_EXPERTS), dtype=jnp.float32) * 0.02
        W1 = jax.random.normal(k2, (N_EXPERTS, D_MODEL, D_FF), dtype=jnp.float32) * 0.02
        b1 = jnp.zeros((N_EXPERTS, D_FF), dtype=jnp.float32)
        W2 = jax.random.normal(k3, (N_EXPERTS, D_FF, D_MODEL), dtype=jnp.float32) * 0.02
        b2 = jnp.zeros((N_EXPERTS, D_MODEL), dtype=jnp.float32)
        return {'x': x, 'gate_w': gate_w, 'W1': W1, 'b1': b1, 'W2': W2, 'b2': b2}
    _L0_ffn_all = _L0_ffn_setup()
    _L0_ffn_in = {k: v for k, v in _L0_ffn_all.items() if k in ('gate_w', 'W1', 'b1', 'W2', 'b2')}
    del _L0_ffn_all

    def _L1_xattn_setup():
        import jax, jax.numpy as jnp
        import numpy as np
        EMB, HEADS = (256, 16)
        HEAD_DIM = EMB // HEADS

        def _linear(x, W, b):
            return jnp.einsum('bse,oe->bso', x, W) + b
        key = jax.random.key(seed)
        ks = jax.random.split(key, 11)
        B, S = (2, 512)
        sc = 1.0 / np.sqrt(EMB)
        inp = {'x': jax.random.normal(ks[0], (B, S, EMB), dtype=jnp.float32), 'y': jax.random.normal(ks[1], (B, S, EMB), dtype=jnp.float32), 'mask': jnp.ones((B, S, S), dtype=jnp.int32), 'Wq': jax.random.normal(ks[2], (EMB, EMB), dtype=jnp.float32) * sc, 'bq': jax.random.normal(ks[3], (EMB,), dtype=jnp.float32) * sc, 'Wk': jax.random.normal(ks[4], (EMB, EMB), dtype=jnp.float32) * sc, 'bk': jax.random.normal(ks[5], (EMB,), dtype=jnp.float32) * sc, 'Wv': jax.random.normal(ks[6], (EMB, EMB), dtype=jnp.float32) * sc, 'bv': jax.random.normal(ks[7], (EMB,), dtype=jnp.float32) * sc, 'Wo': jax.random.normal(ks[8], (EMB, EMB), dtype=jnp.float32) * sc, 'bo': jax.random.normal(ks[9], (EMB,), dtype=jnp.float32) * sc}
        return inp
    _L1_xattn_all = _L1_xattn_setup()
    _L1_xattn_in = {k: v for k, v in _L1_xattn_all.items() if k in ('Wq', 'bq', 'Wk', 'bk', 'Wv', 'bv', 'Wo', 'bo')}
    del _L1_xattn_all

    def _L1_ffn_setup():
        import math
        import jax, jax.numpy as jnp
        import numpy as np
        NUM_EXPERTS = 8
        TOP_K = 2
        CAPACITY_FACTOR = 1.0
        B, S, H, I = (4, 512, 256, 1024)
        key = jax.random.key(seed)
        k_x, k_rw, k_wi, k_wo = jax.random.split(key, 4)
        x = jax.random.normal(k_x, (B, S, H), dtype=jnp.float32)
        lim = math.sqrt(6.0 / (H + NUM_EXPERTS))
        router_w = jax.random.uniform(k_rw, (NUM_EXPERTS, H), minval=-lim, maxval=lim, dtype=jnp.float32)
        router_b = jnp.zeros((NUM_EXPERTS,), dtype=jnp.float32)
        experts_inter = jax.random.normal(k_wi, (NUM_EXPERTS - 1, H, I), dtype=jnp.float32) / math.sqrt(H)
        experts_out = jax.random.normal(k_wo, (NUM_EXPERTS - 1, I, H), dtype=jnp.float32) / math.sqrt(I)
        return {'x': x, 'router_w': router_w, 'router_b': router_b, 'experts_inter': experts_inter, 'experts_out': experts_out}
    _L1_ffn_all = _L1_ffn_setup()
    _L1_ffn_in = {k: v for k, v in _L1_ffn_all.items() if k in ('router_w', 'router_b', 'experts_inter', 'experts_out')}
    del _L1_ffn_all
    return {'x': x, 'ctx_1024': ctx_1024, 'mask_BxSxS2_if1': mask_BxSxS2_if1, 'g_xattn': g_xattn, 'g_ffn': g_ffn, 'L0_xattn_Wq': _L0_xattn_in['Wq'], 'L0_xattn_bq': _L0_xattn_in['bq'], 'L0_xattn_Wk': _L0_xattn_in['Wk'], 'L0_xattn_bk': _L0_xattn_in['bk'], 'L0_xattn_Wv': _L0_xattn_in['Wv'], 'L0_xattn_bv': _L0_xattn_in['bv'], 'L0_xattn_Wo': _L0_xattn_in['Wo'], 'L0_xattn_bo': _L0_xattn_in['bo'], 'L0_ffn_gate_w': _L0_ffn_in['gate_w'], 'L0_ffn_W1': _L0_ffn_in['W1'], 'L0_ffn_b1': _L0_ffn_in['b1'], 'L0_ffn_W2': _L0_ffn_in['W2'], 'L0_ffn_b2': _L0_ffn_in['b2'], 'L1_xattn_Wq': _L1_xattn_in['Wq'], 'L1_xattn_bq': _L1_xattn_in['bq'], 'L1_xattn_Wk': _L1_xattn_in['Wk'], 'L1_xattn_bk': _L1_xattn_in['bk'], 'L1_xattn_Wv': _L1_xattn_in['Wv'], 'L1_xattn_bv': _L1_xattn_in['bv'], 'L1_xattn_Wo': _L1_xattn_in['Wo'], 'L1_xattn_bo': _L1_xattn_in['bo'], 'L1_ffn_router_w': _L1_ffn_in['router_w'], 'L1_ffn_router_b': _L1_ffn_in['router_b'], 'L1_ffn_experts_inter': _L1_ffn_in['experts_inter'], 'L1_ffn_experts_out': _L1_ffn_in['experts_out']}

def reference(x, ctx_1024, mask_BxSxS2_if1, g_xattn, g_ffn, L0_xattn_Wq, L0_xattn_bq, L0_xattn_Wk, L0_xattn_bk, L0_xattn_Wv, L0_xattn_bv, L0_xattn_Wo, L0_xattn_bo, L0_ffn_gate_w, L0_ffn_W1, L0_ffn_b1, L0_ffn_W2, L0_ffn_b2, L1_xattn_Wq, L1_xattn_bq, L1_xattn_Wk, L1_xattn_bk, L1_xattn_Wv, L1_xattn_bv, L1_xattn_Wo, L1_xattn_bo, L1_ffn_router_w, L1_ffn_router_b, L1_ffn_experts_inter, L1_ffn_experts_out):
    import jax
    import jax.numpy as jnp

    def _L0_xattn_ref(query, key, value, Wq, bq, Wk, bk, Wv, bv, Wo, bo):
        import jax, jax.numpy as jnp
        import numpy as np
        EMBED_DIM = 256
        NUM_HEADS = 16
        HEAD_DIM = EMBED_DIM // NUM_HEADS
        B, T_Q, T_K = (2, 512, 512)
        b, tq, _ = query.shape
        tk = key.shape[1]
        q = (query @ Wq.T + bq).reshape(b, tq, NUM_HEADS, HEAD_DIM).transpose(0, 2, 1, 3)
        k = (key @ Wk.T + bk).reshape(b, tk, NUM_HEADS, HEAD_DIM).transpose(0, 2, 1, 3)
        v = (value @ Wv.T + bv).reshape(b, tk, NUM_HEADS, HEAD_DIM).transpose(0, 2, 1, 3)
        scores = jnp.einsum('bhqd,bhkd->bhqk', q, k) / np.sqrt(HEAD_DIM)
        attn = jax.nn.softmax(scores, axis=-1)
        attn = jnp.nan_to_num(attn, nan=0.0)
        out = jnp.einsum('bhqk,bhkd->bhqd', attn, v)
        out = out.transpose(0, 2, 1, 3).reshape(b, tq, EMBED_DIM)
        return out @ Wo.T + bo

    def _L0_ffn_ref(x, gate_w, W1, b1, W2, b2):
        import jax, jax.numpy as jnp
        import numpy as np
        D_MODEL, D_FF, N_EXPERTS, TOP_K = (256, 1024, 8, 2)
        orig_shape = x.shape
        xf = x.reshape(-1, D_MODEL)
        n_tokens = xf.shape[0]
        router_logits = xf @ gate_w
        topk_vals, topk_idx = jax.lax.top_k(router_logits, TOP_K)
        topk_w = jax.nn.softmax(topk_vals, axis=-1)
        comb = jnp.zeros((n_tokens, N_EXPERTS), dtype=x.dtype)
        comb = comb.at[jnp.arange(n_tokens)[:, None], topk_idx].add(topk_w)
        h = jax.nn.gelu(jnp.einsum('nd,edf->enf', xf, W1) + b1[:, None, :], approximate=False)
        y = jnp.einsum('enf,efd->end', h, W2) + b2[:, None, :]
        out = jnp.einsum('ne,end->nd', comb, y)
        return out.reshape(orig_shape)

    def _L1_xattn_ref(x, y, mask, Wq, bq, Wk, bk, Wv, bv, Wo, bo):
        import jax, jax.numpy as jnp
        import numpy as np
        EMB, HEADS = (256, 16)
        HEAD_DIM = EMB // HEADS

        def _linear(x, W, b):
            return jnp.einsum('bse,oe->bso', x, W) + b
        B, S, _ = x.shape
        q = _linear(x, Wq, bq).reshape(B, S, HEADS, HEAD_DIM).transpose(0, 2, 1, 3)
        k = _linear(y, Wk, bk).reshape(B, -1, HEADS, HEAD_DIM).transpose(0, 2, 1, 3)
        v = _linear(y, Wv, bv).reshape(B, -1, HEADS, HEAD_DIM).transpose(0, 2, 1, 3)
        score = jnp.einsum('bhqd,bhkd->bhqk', q, k) / jnp.sqrt(jnp.float32(HEAD_DIM))
        weights = jax.nn.softmax(score, axis=-1)
        attn = jnp.einsum('bhqk,bhkd->bhqd', weights, v)
        attn = attn.transpose(0, 2, 1, 3).reshape(B, S, EMB)
        return _linear(attn, Wo, bo)

    def _L1_ffn_ref(x, router_w, router_b, experts_inter, experts_out):
        import math
        import jax, jax.numpy as jnp
        import numpy as np
        NUM_EXPERTS = 8
        TOP_K = 2
        CAPACITY_FACTOR = 1.0
        B, S, H, I = (4, 512, 256, 1024)
        batch, seq, hidden = x.shape
        n_exp = router_w.shape[0]
        n_tok = batch * seq
        cap = math.ceil(n_tok / n_exp * CAPACITY_FACTOR)
        logits = jnp.einsum('bsh,eh->bse', x, router_w) + router_b
        weights_flat = jax.nn.softmax(logits, axis=-1).reshape(n_tok, n_exp)
        x_flat = x.reshape(n_tok, hidden)
        topk_vals, topk_idx = jax.lax.top_k(weights_flat, TOP_K)
        rows = jnp.arange(n_tok)[:, None]
        topk_flat = jnp.zeros_like(weights_flat).at[rows, topk_idx].set(topk_vals)
        routing_mask = (topk_flat > 0).astype(jnp.int32)
        noop_w = topk_flat[:, -1]
        noop_mask = routing_mask[:, -1].astype(x.dtype)
        expert_w = topk_flat[:, :-1]
        expert_mask = routing_mask[:, :-1]
        sorted_indices = jnp.argsort(-expert_mask, axis=0)[:cap]
        sorted_mask = jnp.take_along_axis(expert_mask, sorted_indices, axis=0)
        used_idx = (sorted_indices * sorted_mask).reshape(-1)
        inputs = x_flat[used_idx] * sorted_mask.reshape(-1).astype(x.dtype)[:, None]
        inputs = inputs.reshape(cap, n_exp - 1, hidden)
        in_w = jnp.take_along_axis(expert_w, sorted_indices, axis=0)
        h = jax.nn.relu(jnp.einsum('ceh,ehi->cei', inputs, experts_inter))
        out = jnp.einsum('cei,eih->ceh', h, experts_out) * in_w[..., None]
        combined = jnp.zeros_like(x_flat).at[used_idx].add(out.reshape(-1, hidden))
        combined = combined + x_flat * (noop_w * noop_mask)[:, None]
        return combined.reshape(batch, seq, hidden)
    x = x + jnp.tanh(g_xattn[0]) * _L0_xattn_ref(_layernorm(x, axis=-1), ctx_1024, ctx_1024, L0_xattn_Wq, L0_xattn_bq, L0_xattn_Wk, L0_xattn_bk, L0_xattn_Wv, L0_xattn_bv, L0_xattn_Wo, L0_xattn_bo)
    x = x + jnp.tanh(g_ffn[0]) * _L0_ffn_ref(_layernorm(x, axis=-1), L0_ffn_gate_w, L0_ffn_W1, L0_ffn_b1, L0_ffn_W2, L0_ffn_b2)
    x = x + jnp.tanh(g_xattn[1]) * _L1_xattn_ref(_layernorm(x, axis=-1), ctx_1024, mask_BxSxS2_if1, L1_xattn_Wq, L1_xattn_bq, L1_xattn_Wk, L1_xattn_bk, L1_xattn_Wv, L1_xattn_bv, L1_xattn_Wo, L1_xattn_bo)
    x = x + jnp.tanh(g_ffn[1]) * _L1_ffn_ref(_layernorm(x, axis=-1), L1_ffn_router_w, L1_ffn_router_b, L1_ffn_experts_inter, L1_ffn_experts_out)
    return x

_drawn_inputs = setup_inputs


def setup_inputs(seed=0):
    import zlib

    import numpy as np

    out = dict(_drawn_inputs(seed))
    spreads = {'g_ffn': (-1.0, 0.6),
     'L0_xattn_bq': (0.0, 0.278),
     'L0_xattn_bk': (0.0, 0.8),
     'L0_xattn_bv': (0.0, 0.1),
     'L0_xattn_bo': (0.0, 0.1),
     'L0_ffn_b1': (0.0, 0.326),
     'L0_ffn_b2': (0.0, 0.1),
     'L1_ffn_router_b': (0.0, 0.1)}
    factors = {'L1_xattn_bq': 3.387, 'L1_xattn_bk': 8.0}
    for name, (base, spread) in spreads.items():
        noise = np.random.default_rng([zlib.crc32(name.encode()), seed]).standard_normal(out[name].shape)
        drawn = base * np.exp(spread * noise) if base else spread * noise
        out[name] = jnp.asarray(drawn.astype(out[name].dtype))
    for name, factor in factors.items():
        out[name] = (out[name] * factor).astype(out[name].dtype)
    return out
```

```python
from contextlib import ExitStack

import concourse.bass as bass
from concourse import mybir

F32 = mybir.dt.float32
F32R = mybir.dt.float32r
I32 = mybir.dt.int32
U32 = mybir.dt.uint32
ALU = mybir.AluOpType
ACT = mybir.ActivationFunctionType
AX = mybir.AxisListType

P = 128
B, S, D = 8, 256, 256
N = B * S
TT = N // P
QT = S // P
KC = D // P
H, HD = 16, 16
HG = 4
CH = H // HG
GROUPS = H // HG
RING = 4
BY_POOL = (2, 4, 5, 7)
EPS = 1e-5
BF16 = mybir.dt.bfloat16
E, F = 8, 1024
FC = F // P
SB = 256
L0_BLOCKS = (2 * N + E * (SB - 1)) // SB
SLOTS = L0_BLOCKS * SB
CT = 4
LAYERS = (0, 1)


def spread(ap, axis, n):
    shape = list(ap.shape)
    return ap.unsqueeze(axis).broadcast_to(shape[:axis] + [n] + shape[axis:])


def wait(eng, sem, value):
    if isinstance(value, int) and value <= 0:
        return
    eng.wait_ge(sem, value)


def wait_apart(eng, sem, value, passed):
    eng.wait_ge(sem, value)
    eng.sem_inc(passed, 1)


def semaphores(nc, ctx):
    taken = []

    def clear():
        nc.clear_and_free_semaphores(taken)
        nc.all_engine_barrier()

    def sem(name):
        taken.append(nc.alloc_semaphore(name))
        return taken[-1]

    ctx.callback(clear)
    return sem


def split_matmul(pe, out, lhs, rhs, start, stop):
    pe.matmul(out, lhs[0], rhs[0], start=start, stop=False)
    pe.matmul(out, lhs[1], rhs[0], start=False, stop=False)
    return pe.matmul(out, lhs[0], rhs[1], start=False, stop=stop)


def attention_phase(nc, layer, shared, dram, load_x):
    x, ident, tanh_g = shared["x"], shared["ident"], shared["tanh_g"]
    tg = tanh_g[:, layer:layer + 1]

    with ExitStack() as ctx:
        def sb(name, shape, dt=F32):
            return ctx.enter_context(nc.sbuf_tensor(f"{name}_a{layer}", shape, dt))

        def ps(name, shape):
            return ctx.enter_context(nc.psum_tensor(f"{name}_a{layer}", shape, F32))

        new_sem = semaphores(nc, ctx)

        def sem(name):
            return new_sem(f"{name}_a{layer}")

        wq_raw, wk_raw = sb("wq_raw", [P, KC, D]), sb("wk_raw", [P, KC, D])
        wv_raw, wo_raw = sb("wv_raw", [P, KC, D]), sb("wo_raw", [P, KC, D])
        wq = [sb(f"wq{i}", [P, KC, CH * P], F32R) for i in range(2)]
        wk = [sb(f"wk{i}", [P, KC, CH * P], F32R) for i in range(2)]
        wv = [sb(f"wv{i}", [P, KC, D], F32R) for i in range(2)]
        wo = [sb(f"wo{i}", [P, KC, D], F32R) for i in range(2)]
        bq, bk = sb("bq", [P, CH]), sb("bk", [P, CH])
        bv, bo = sb("bv", [P, D]), sb("bo", [P, D])
        tgbo = sb("tgbo", [P, D])
        minus_half, eps_col = sb("minus_half", [P, QT]), sb("eps_col", [P, 1])
        lane = sb("lane", [P, H], I32)
        lane_low = sb("lane_low", [P, H], I32)
        is_head = sb("is_head", [P, H])
        low_bit = sb("low_bit", [P, 1], I32)
        minus_low = sb("minus_low", [P, 1])
        head_row = sb("head_row", [P, H, P], F32R)

        ctx_raw = [sb(f"ctx_raw{i}", [P, KC, S]) for i in range(2)]
        ctx_t = [sb(f"ctx_t{i}", [P, KC, S], F32R) for i in range(2)]
        stats, mean_var = sb("stats", [P, QT, 6]), sb("mean_var", [P, QT, 2])
        var_eps, rstd = sb("var_eps", [P, QT]), sb("rstd", [P, QT])
        xn = sb("xn", [P, QT, D])
        xn_t = [sb(f"xn_t{i}", [P, KC, S], F32R) for i in range(2)]
        q_full, k_full = sb("q_full", [P, CH, S]), sb("k_full", [P, CH, S])
        q_high = sb("q_high", [P, CH, S], F32R)
        q_st = [sb(f"q_st{i}", [P, CH, S], F32R) for i in range(2)]
        k_hi = [sb(f"k_hi{i}", [P, CH, S], F32R) for i in range(2)]
        k_lo = [sb(f"k_lo{i}", [P, CH, S], F32R) for i in range(2)]
        v_full = sb("v_full", [P, QT, H, HD])
        v = [sb(f"v{i}", [P, QT, H, P], F32R) for i in range(2)]
        mx = sb("mx", [P, H, QT])
        m_rep = sb("m_rep", [P, QT, HG, 2, H])
        m_t = sb("m_t", [P, S], F32R)
        prob = [sb(f"prob{i}", [P, 2, QT, S]) for i in range(2)]
        prob_hi = [sb(f"prob_hi{i}", [P, 2, QT, S], F32R) for i in range(RING)]
        prob_lo = [sb(f"prob_lo{i}", [P, 2, QT, S], F32R) for i in range(RING)]
        head_t = [sb(f"head_t{i}", [P, S]) for i in range(2)]
        rsum, o = sb("rsum", [P, QT, HG]), sb("o", [P, QT, D])
        o_t = [sb(f"o_t{i}", [P, KC, S], F32R) for i in range(2)]

        ps_st = [ps(f"ps_st{i}", [P, 2, QT, S]) for i in range(2)]
        bank_a, bank_b = ps("bank_a", [P, 512]), ps("bank_b", [P, 512])
        ps_head = ps("ps_head", [P, 512])
        ps_o = ps("ps_o", [P, 4, HG, 32])

        w_ld, q_ld, rest_ld = sem("w_ld"), sem("q_ld"), sem("rest_ld")
        x_ld = [sem("x_ld0"), sem("x_ld1")]
        ctx_ld = [sem("ctx_ld0"), sem("ctx_ld1")]
        pool_const, dve_const, wq_ready, wk_ready, wv_ready, wo_ready, tgbo_ready = (
            sem(n) for n in ("pool_const", "dve_const", "wq_ready", "wk_ready", "wv_ready", "wo_ready", "tgbo_ready"))
        dve_passed, pool_passed = sem("dve_passed"), sem("pool_passed")
        wq_hi, wk_hi, wv_hi, wo_hi = sem("wq_hi"), sem("wk_hi"), sem("wv_hi"), sem("wo_hi")
        ln_stats, ln_mean, ln_eps, ln_rstd, xn_ready = (
            sem(n) for n in ("ln_stats", "ln_mean", "ln_eps", "ln_rstd", "xn_ready"))
        bias_added, ctx_hi, ctx_ready = sem("bias_added"), sem("ctx_hi"), sem("ctx_ready")
        xt_ps, xt_hi, xt_ready = sem("xt_ps"), sem("xt_hi"), sem("xt_ready")
        q_ps, q_biased, q_rounded, q_ready = sem("q_ps"), sem("q_biased"), sem("q_rounded"), sem("q_ready")
        k_ps, k_biased, k_rounded, k_ready = sem("k_ps"), sem("k_biased"), sem("k_rounded"), sem("k_ready")
        v_ps, v_ready = sem("v_ps"), sem("v_ready")
        s_ps, max_done, m_hi, m_ready, mt_ps, mt_ready = (
            sem(n) for n in ("s_ps", "max_done", "m_hi", "m_ready", "mt_ps", "mt_ready"))
        prob_full, lo_dve, lo_pool, v_full_ready, v_rounded = (
            sem(n) for n in ("prob_full", "lo_dve", "lo_pool", "v_full_ready", "v_rounded"))
        st_ps, prob_ready, pv_done, head_out, turned, summed, sum_inv, o_ready = (
            sem(n) for n in ("st_ps", "prob_ready", "pv_done", "head_out", "turned", "summed", "sum_inv", "o_ready"))
        ot_ps, ot_hi, ot_ready, out_ps, x_done = (
            sem(n) for n in ("ot_ps", "ot_hi", "ot_ready", "out_ps", "x_done"))

        def x_tiles(b):
            return x[:, bass.ds(b * QT, QT), :] if not isinstance(b, int) else x[:, b * QT:b * QT + QT, :]

        PER_POOL = len(BY_POOL)
        PER_DVE = H // 2 - PER_POOL

        def split_wait(eng, b, j):
            if j < 0:
                b, j = b - 1, j + H // 2
            if j in BY_POOL:
                wait(eng, lo_pool, b * PER_POOL + BY_POOL.index(j) + 1)
            else:
                wait(eng, lo_dve, b * PER_DVE + sum(i not in BY_POOL for i in range(j)) + 1)

        def split_prob(eng, b, j):
            eng.wait_ge(prob_ready, b * 8 + j + 1)
            wait(eng, pv_done, b * 8 + j - RING + 1)
            eng.tensor_tensor(prob_lo[j % RING][:, :, :, :], prob[j % 2][:, :, :, :],
                              prob_hi[j % RING][:, :, :, :].bitcast(F32),
                              ALU.subtract).then_inc(lo_pool if j in BY_POOL else lo_dve, 1)

        block = ctx.enter_context(nc.Block())

        @block.sync
        def _(sp):
            if load_x:
                src = dram["x"].rearrange("(t p) d -> p t d", p=P)
                sp.dma_start(x[:, 0:QT, :], src[:, 0:QT, :]).then_inc(x_ld[0], 16)
            w3 = [dram[n].rearrange("(k p) n -> p k n", p=P) for n in ("wq", "wk", "wv", "wo")]
            sp.dma_start(wq_raw[:, :, :], w3[0]).then_inc(q_ld, 16)
            sp.dma_start(bq[:, :], dram["bq"]).then_inc(q_ld, 16)
            sp.dma_start(bk[:, :], dram["bk"]).then_inc(w_ld, 16)
            sp.dma_start(wk_raw[:, :, :], w3[1]).then_inc(w_ld, 16)
            ctx_src = dram["ctx_t"].rearrange("(k p) n -> p k n", p=P)
            sp.dma_start(ctx_raw[0][:, :, :], ctx_src[:, :, 0:S]).then_inc(ctx_ld[0], 16)
            sp.dma_start(wv_raw[:, :, :], w3[2]).then_inc(rest_ld, 16)
            sp.dma_start(wo_raw[:, :, :], w3[3]).then_inc(rest_ld, 16)
            sp.dma_start(bv[:, :], dram["bv"]).then_inc(rest_ld, 16)
            sp.dma_start(bo[:, :], dram["bo"]).then_inc(rest_ld, 16)
            if load_x:
                sp.dma_start(x[:, QT:TT, :], src[:, QT:TT, :]).then_inc(x_ld[1], 16)
            sp.dma_start(ctx_raw[1][:, :, :], ctx_src[:, :, S:2 * S]).then_inc(ctx_ld[1], 16)
            with sp.Fori(1, B // 2) as t:
                for i in range(2):
                    sp.wait_ge(ctx_ready, t * 2 - 1 + i)
                    sp.dma_start(ctx_raw[i][:, :, :], ctx_src[:, :, bass.ds(t * (2 * S) + i * S, S)]).then_inc(ctx_ld[i], 16)

        @block.gpsimd
        def _(pool):
            pool.memset(minus_half[:, :], -0.5).then_inc(pool_const, 1)
            pool.iota(lane[:, :], pattern=[[-1, H]], base=H, channel_multiplier=1).then_inc(pool_const, 1)

            def inverse_deviation(b):
                wait_apart(pool, ln_mean, b * QT + QT, pool_passed)
                pool.tensor_scalar(var_eps[:, :], mean_var[:, :, 1], EPS, None, ALU.add).then_inc(ln_eps, 1)
                pool.wait_ge(ln_eps, b + 1)
                pool.tensor_tensor(rstd[:, :], var_eps[:, :], minus_half[:, :], ALU.pow).then_inc(ln_rstd, 1)

            def add_bias(b):
                pool.wait_ge(xn_ready, b * QT + QT)
                pool.wait_ge(tgbo_ready, 1)
                pool.tensor_tensor(x_tiles(b), x_tiles(b), spread(tgbo[:, :], 1, QT), ALU.add).then_inc(bias_added, 1)

            def context_high(b, par, half):
                wait(pool, v_ps, b)
                wait_apart(pool, ctx_ld[par], (half + 1) * 16, pool_passed)
                pool.tensor_copy(ctx_t[0][:, :, :], ctx_raw[par][:, :, :]).then_inc(ctx_hi, 1)

            def context_low(b, par):
                pool.wait_ge(ctx_hi, b + 1)
                pool.tensor_tensor(ctx_t[1][:, :, :], ctx_raw[par][:, :, :], ctx_t[0][:, :, :].bitcast(F32),
                                   ALU.subtract).then_inc(ctx_ready, 1)

            def of_group(part, g):
                return part[:, :, :, :].rearrange("p k (c g) n -> p k c g n", g=HG)[:, :, :, g, :]

            def keys_low(b, par):
                wait(pool, pv_done, (b - 1) * 8)
                for u in range(2):
                    cs = slice(2 * u, 2 * u + 2)
                    pool.wait_ge(k_rounded, b * 2 + u + 1)
                    pool.tensor_tensor(k_lo[par][:, cs, :], k_full[:, cs, :], k_hi[par][:, cs, :].bitcast(F32),
                                       ALU.subtract).then_inc(k_ready, 1)

            def values(b):
                wait(pool, pv_done, b * 8)
                wait_apart(pool, v_full_ready, b + 1, pool_passed)
                for g in range(HG):
                    full = v_full[:, :, :, :].rearrange("p k (c g) d -> p k c g d", g=HG)[:, :, :, g, :]
                    high, low = (of_group(v[i], g)[:, :, :, 32 * g:32 * g + HD] for i in range(2))
                    pool.tensor_copy(high, full).then_inc(v_rounded, 1)
                    pool.wait_ge(v_rounded, b * HG + g + 1)
                    ins = pool.tensor_tensor(low, full, high.bitcast(F32), ALU.subtract)
                ins.then_inc(v_ready, 1)

            def body(b, par, half, more=True, last=False):
                if more:
                    inverse_deviation(b)
                if not last:
                    keys_low(b - 1, 1 - par)
                split_prob(pool, b - 2, BY_POOL[0])
                if more:
                    add_bias(b)
                split_prob(pool, b - 2, BY_POOL[1])
                if more:
                    context_high(b, par, half)
                split_prob(pool, b - 2, BY_POOL[2])
                if more:
                    context_low(b, par)
                split_prob(pool, b - 2, BY_POOL[3])
                if not last:
                    values(b - 1)

            for i in range(2):
                pool.memset(v[i][:, :, :, :].bitcast(F32), 0.0).then_inc(pool_const, 1)
            pool.wait_ge(pool_const, 4)
            for g in range(HG):
                pool.memset(of_group(v[0], g)[:, :, :, 32 * g + HD:32 * g + HD + 1].bitcast(F32), 1.0).then_inc(pool_const, 1)
            context_high(0, 0, 0)
            context_low(0, 0)
            inverse_deviation(0)
            add_bias(0)
            keys_low(0, 0)
            values(0)
            inverse_deviation(1)
            add_bias(1)
            context_high(1, 1, 0)
            context_low(1, 1)
            body(2, 0, 1)
            with pool.Fori(1, B // 2 - 1) as t:
                body(t * 2 + 1, 1, t)
                body(t * 2 + 2, 0, t + 1)
            body(B - 1, 1, B // 2 - 1)
            body(B, 0, None, more=False)
            body(B + 1, 1, None, more=False, last=True)

        @block.scalar
        def _(act):
            def project(b, u, ps_sem, done_sem, consumed, bias, full):
                bank = bank_a if u else bank_b
                act.wait_ge(ps_sem, b * 2 + u + 1)
                wait(act, consumed, b * 2 + u - 1)
                for c in range(2):
                    ins = act.activation(full[:, 2 * u + c, :], bank[:, c * S:(c + 1) * S], ACT.Identity,
                                         bias=bias[:, 2 * u + c:2 * u + c + 1])
                ins.then_inc(done_sem, 1)

            def queries(b, u):
                project(b, u, q_ps, q_biased, q_ready, bq, q_full)

            def keys(b):
                for u in range(2):
                    project(b, u, k_ps, k_biased, k_ready, bk, k_full)

            def inputs(b):
                act.wait_ge(xt_ps, b + 1)
                act.activation(xn_t[0][:, :, :], bank_a[:, :].rearrange("p (k s) -> p k s", k=KC),
                               ACT.Copy).then_inc(xt_hi, 1)

            def maxima(b):
                act.wait_ge(mt_ps, b + 1)
                act.activation(m_t[:, :], bank_b[:, 0:S], ACT.Copy).then_inc(mt_ready, 1)

            def out_hi(b):
                act.wait_ge(ot_ps, b + 1)
                act.activation(o_t[0][:, :, :], bank_a[:, :].rearrange("p (k s) -> p k s", k=KC),
                               ACT.Copy).then_inc(ot_hi, 1)

            def probabilities(b, j):
                act.wait_ge(st_ps, b * 8 + j + 1)
                split_wait(act, b, j - 2)
                act.activation(prob[j % 2][:, :, :, :], ps_st[j % 2][:, :, :, :], ACT.Exp,
                               scale=HD ** -0.5).then_inc(prob_full, 1)
                wait(act, pv_done, b * 8 + j - RING + 1)
                act.activation(prob_hi[j % RING][:, :, :, :], ps_st[j % 2][:, :, :, :], ACT.Exp,
                               scale=HD ** -0.5).then_inc(prob_ready, 1)

            def head_copy(b, g):
                act.wait_ge(pv_done, b * 8 + 2 * g + 2)
                wait(act, turned, b * GROUPS + g - 1)
                act.activation(head_t[g % 2][:, :], ps_head[:, 0:S], ACT.Copy).then_inc(head_out, 1)

            def body(b, first=False, last=False):
                if not last:
                    inputs(b + 1)
                maxima(b)
                if not last:
                    queries(b + 1, 0)
                if not first:
                    out_hi(b - 1)
                probabilities(b, 0)
                if not last:
                    queries(b + 1, 1)
                    keys(b + 1)
                probabilities(b, 1)
                for j in range(2, H // 2):
                    probabilities(b, j)
                    if j % 2:
                        head_copy(b, (j - 3) // 2)
                head_copy(b, GROUPS - 1)

            act.wait_ge(q_ld, 32)
            act.wait_ge(w_ld, 32)
            inputs(0)
            queries(0, 0)
            queries(0, 1)
            keys(0)
            body(0, first=True)
            with act.Fori(1, B - 1) as b:
                body(b)
            body(B - 1, last=True)
            out_hi(B - 1)

        @block.vector
        def _(dve):
            def spread_weight(raw, parts, hi_sem, ready_sem):
                for k in range(KC):
                    src = raw[:, k, :].rearrange("p (h d) -> p h d", d=HD)
                    for r in range(2):
                        ins = dve.tensor_copy(parts[0][:, k, :].rearrange("p (h r d) -> p h r d", r=2, d=HD)[:, :, r, :], src)
                ins.then_inc(hi_sem, 1)
                dve.wait_ge(hi_sem, 1)
                for k in range(KC):
                    src = raw[:, k, :].rearrange("p (h d) -> p h d", d=HD)
                    for r in range(2):
                        hi, lo = (w[:, k, :].rearrange("p (h r d) -> p h r d", r=2, d=HD)[:, :, r, :] for w in parts)
                        ins = dve.tensor_tensor(lo, src, hi.bitcast(F32), ALU.subtract)
                ins.then_inc(ready_sem, 1)

            def weight(raw, parts, hi_sem, ready_sem):
                dve.tensor_copy(parts[0][:, :, :], raw[:, :, :]).then_inc(hi_sem, 1)
                dve.wait_ge(hi_sem, 1)
                dve.tensor_tensor(parts[1][:, :, :], raw[:, :, :], parts[0][:, :, :].bitcast(F32),
                                  ALU.subtract).then_inc(ready_sem, 1)

            def moments(b):
                for q in range(QT):
                    dve.bn_stats(stats[:, q, :], x_tile(b, q)).then_inc(ln_stats, 1)
                wait_apart(dve, ln_stats, b * QT + QT, dve_passed)
                for q in range(QT):
                    dve.bn_aggr(mean_var[:, q, :], stats[:, q, :]).then_inc(ln_mean, 1)

            def normalise_rows(b):
                dve.wait_ge(ln_rstd, b + 1)
                wait(dve, xt_ps, b)
                for q in range(QT):
                    dve.tensor_scalar(xn[:, q:q + 1, :], x_tile(b, q), mean_var[:, q, 0:1], rstd[:, q:q + 1],
                                      ALU.subtract, ALU.mult).then_inc(xn_ready, 1)

            def x_tile(b, q):
                return x[:, bass.ds(b * QT + q, 1), :] if not isinstance(b, int) else x[:, b * QT + q:b * QT + q + 1, :]

            def low_part(full, parts, hi_sem, done_sem, count):
                dve.wait_ge(hi_sem, count)
                dve.tensor_tensor(parts[1][:, :, :], full[:, :].rearrange("p (k s) -> p k s", k=KC),
                                  parts[0][:, :, :].bitcast(F32), ALU.subtract).then_inc(done_sem, 1)

            def queries(b, par, u):
                cs = slice(2 * u, 2 * u + 2)
                dve.wait_ge(q_biased, b * 2 + u + 1)
                dve.tensor_copy(q_high[:, cs, :], q_full[:, cs, :]).then_inc(q_rounded, 1)
                dve.wait_ge(q_rounded, b * 2 + u + 1)
                dve.scalar_tensor_tensor(q_st[par][:, cs, :], q_high[:, cs, :].bitcast(F32), minus_low[:, 0:1],
                                         q_full[:, cs, :], ALU.mult, ALU.add).then_inc(q_ready, 1)

            def keys(b, par):
                for u in range(2):
                    cs = slice(2 * u, 2 * u + 2)
                    dve.wait_ge(k_biased, b * 2 + u + 1)
                    dve.tensor_copy(k_hi[par][:, cs, :], k_full[:, cs, :]).then_inc(k_rounded, 1)

            def values(b, par):
                dve.wait_ge(v_ps, b + 1)
                wait(dve, v_ready, b)
                for kt in range(QT):
                    ins = dve.tensor_tensor(v_full[:, kt, :, :],
                                            bank_a[:, kt * D:(kt + 1) * D].rearrange("p (h d) -> p h d", d=HD),
                                            bv[:, :].rearrange("p (h d) -> p h d", d=HD), ALU.add)
                ins.then_inc(v_full_ready, 1)

            def take_maxima(b, i):
                for h in (2 * i, 2 * i + 1):
                    dve.wait_ge(s_ps, b * H + h + 1)
                    bank = bank_a if h % 2 else bank_b
                    dve.tensor_reduce(mx[:, h, :], bank[:, :].rearrange("p (q s) -> p q s", q=QT), AX.X,
                                      ALU.max).then_inc(max_done, 1)

            def heads(b, last, more):
                for j in range(2, H // 2):
                    if j - 1 not in BY_POOL:
                        split_prob(dve, b, j - 1)
                    if j == 2 and more:
                        normalise_rows(b + 2)
                    if j >= 5 and j % 2:
                        normalise(b, (j - 5) // 2)
                    if not last:
                        take_maxima(b + 1, j - 1)
                if not last:
                    take_maxima(b + 1, H // 2 - 1)
                    negate(b + 1)
                normalise(b, GROUPS - 2)

            def negate(b):
                dve.wait_ge(max_done, b * H + H)
                src = spread(mx[:, :, :].rearrange("p h q -> p q h"), 2, HG)
                dve.tensor_scalar(m_rep[:, :, :, 0, :].bitcast(F32R), src, -1.0, None, ALU.mult).then_inc(m_hi, 1)
                dve.wait_ge(m_hi, b + 1)
                for q in range(QT):
                    ins = dve.scalar_tensor_tensor(m_rep[:, q, :, 1, :], src[:, q, :, :], -1.0, m_rep[:, q, :, 0, :],
                                                   ALU.mult, ALU.subtract)
                ins.then_inc(m_ready, 1)

            def normalise(b, g):
                dve.wait_ge(turned, b * GROUPS + g + 1)
                tiles = slice(g % 2 * QT, g % 2 * QT + QT)
                dve.reciprocal(rsum[:, :, :], ps_o[:, tiles, :, HD]).then_inc(sum_inv, 1)
                dve.wait_ge(sum_inv, b * GROUPS + g + 1)
                if g == 0:
                    wait(dve, ot_ps, b)
                for q in range(QT):
                    ins = dve.tensor_tensor(o[:, q, g * HG * HD:(g + 1) * HG * HD].rearrange("p (h d) -> p h d", d=HD),
                                            ps_o[:, g % 2 * QT + q, :, 0:HD], spread(rsum[:, q, :], 2, HD), ALU.mult)
                ins.then_inc(o_ready, 1)

            def residual(b):
                dve.wait_ge(out_ps, b + 1)
                dve.wait_ge(bias_added, b + 1)
                dve.scalar_tensor_tensor(x_tiles(b), bank_b[:, :].rearrange("p (q d) -> p q d", q=QT), tg, x_tiles(b),
                                         ALU.mult, ALU.add).then_inc(x_done, 1)

            def body(b, par, first=False, last=False):
                if not last:
                    low_part(bank_a, xn_t, xt_hi, xt_ready, b + 2)
                if not first:
                    normalise(b - 1, GROUPS - 1)
                if not last:
                    queries(b + 1, 1 - par, 0)
                if not first:
                    low_part(bank_a, o_t, ot_hi, ot_ready, b)
                if not last:
                    queries(b + 1, 1 - par, 1)
                    keys(b + 1, 1 - par)
                if not first:
                    residual(b - 1)
                if not last:
                    values(b + 1, 1 - par)
                more = not (isinstance(b, int) and b + 2 >= B)
                split_prob(dve, b, 0)
                if not last:
                    take_maxima(b + 1, 0)
                if more:
                    moments(b + 2)
                heads(b, last, more)

            if load_x:
                dve.wait_ge(x_ld[0], 16)
            moments(0)
            normalise_rows(0)
            dve.wait_ge(q_ld, 32)
            spread_weight(wq_raw, wq, wq_hi, wq_ready)
            dve.wait_ge(w_ld, 32)
            spread_weight(wk_raw, wk, wk_hi, wk_ready)
            dve.wait_ge(pool_const, 2)
            dve.tensor_scalar(lane_low[:, :], lane[:, :], 15, None, ALU.bitwise_and).then_inc(dve_const, 1)
            dve.tensor_scalar(low_bit[:, :], lane[:, 0:1], 16, None, ALU.bitwise_and).then_inc(dve_const, 1)
            dve.wait_ge(dve_const, 2)
            dve.tensor_scalar(is_head[:, :], lane_low[:, :], 0.0, None, ALU.is_equal).then_inc(dve_const, 1)
            dve.tensor_scalar(minus_low[:, :], low_bit[:, :], 1.0 / 16, -1.0, ALU.mult, ALU.add).then_inc(dve_const, 1)
            dve.wait_ge(dve_const, 4)
            dve.tensor_copy(head_row[:, :, :], spread(is_head[:, :], 2, P)).then_inc(dve_const, 1)
            low_part(bank_a, xn_t, xt_hi, xt_ready, 1)
            dve.wait_ge(rest_ld, 64)
            weight(wv_raw, wv, wv_hi, wv_ready)
            dve.tensor_scalar(tgbo[:, :], bo[:, :], tg, None, ALU.mult).then_inc(tgbo_ready, 1)
            queries(0, 0, 0)
            queries(0, 0, 1)
            keys(0, 0)
            values(0, 0)
            if load_x:
                dve.wait_ge(x_ld[1], 16)
            moments(1)
            normalise_rows(1)
            for i in range(H // 2):
                take_maxima(0, i)
            negate(0)
            weight(wo_raw, wo, wo_hi, wo_ready)
            body(0, 0, first=True)
            with dve.Fori(0, B // 2 - 2) as t:
                body(t * 2 + 1, 1)
                body(t * 2 + 2, 0)
            body(B - 3, 1)
            body(B - 2, 0)
            body(B - 1, 1, last=True)
            normalise(B - 1, GROUPS - 1)
            low_part(bank_a, o_t, ot_hi, ot_ready, B)
            residual(B - 1)

        @block.tensor
        def _(pe):
            def turn(src, bank):
                for q in range(QT):
                    for k in range(KC):
                        ins = pe.transpose(bank[:, k * S + q * P:k * S + (q + 1) * P], src[:, q, k * P:(k + 1) * P], ident[:, :])
                return ins

            def x_transpose(b):
                pe.wait_ge(xn_ready, b * QT + QT)
                wait(pe, max_done, b * H)
                turn(xn, bank_a).then_inc(xt_ps, 1)

            def max_transpose(b):
                pe.wait_ge(m_ready, b + 1)
                for q in range(QT):
                    ins = pe.transpose(bank_b[:, q * P:(q + 1) * P],
                                       m_rep[:, q, :, :, :].rearrange("p g r h -> p (g r h)"), ident[:, :])
                ins.then_inc(mt_ps, 1)

            def o_transpose(b, x_next):
                pe.wait_ge(o_ready, (b + 1) * GROUPS)
                if x_next is None:
                    wait(pe, ot_ready, b)
                else:
                    pe.wait_ge(xt_ready, x_next + 1)
                turn(o, bank_a).then_inc(ot_ps, 1)

            def heads_project(w, src, bank, u, done):
                for c in range(2):
                    for k in range(KC):
                        cols = slice((2 * u + c) * P, (2 * u + c + 1) * P)
                        ins = split_matmul(pe, bank[:, c * S:(c + 1) * S], [w[i][:, k, cols] for i in range(2)],
                                           [src[i][:, k, :] for i in range(2)], k == 0, k == KC - 1)
                ins.then_inc(done, 1)

            def queries(b, u, first=False):
                if u == 0:
                    pe.wait_ge(xt_ready, b + 1)
                    wait(pe, mt_ready, b)
                elif not first:
                    pe.wait_ge(ot_ready, b - 1)
                heads_project(wq, xn_t, bank_a if u else bank_b, u, q_ps)

            def keys(b):
                pe.wait_ge(ctx_ready, b + 1)
                pe.wait_ge(q_biased, b * 2 + 1)
                heads_project(wk, ctx_t, bank_b, 0, k_ps)
                pe.wait_ge(q_biased, b * 2 + 2)
                heads_project(wk, ctx_t, bank_a, 1, k_ps)

            def token_major(parts, w, bank, done):
                for q in range(QT):
                    for k in range(KC):
                        ins = split_matmul(pe, bank[:, q * D:(q + 1) * D],
                                           [parts[i][:, k, q * P:(q + 1) * P] for i in range(2)],
                                           [w[i][:, k, :] for i in range(2)], k == 0, k == KC - 1)
                ins.then_inc(done, 1)

            def out_project(b, k_next):
                pe.wait_ge(ot_ready, b + 1)
                if k_next is None:
                    wait(pe, x_done, b)
                else:
                    pe.wait_ge(k_biased, k_next * 2 + 1)
                token_major(o_t, wo, bank_b, out_ps)

            def value_project(b):
                pe.wait_ge(k_biased, b * 2 + 2)
                token_major(ctx_t, wv, bank_a, v_ps)

            def head_scores(b, par, i):
                for h in (2 * i, 2 * i + 1):
                    bank = bank_a if h % 2 else bank_b
                    if h == 0:
                        pe.wait_ge(q_ready, b * 2 + 2)
                        pe.wait_ge(k_rounded, b * 2 + 2)
                        wait(pe, x_done, b - 1)
                    elif h == 1:
                        pe.wait_ge(v_full_ready, b + 1)
                    else:
                        pe.wait_ge(max_done, b * H + h - 1)
                    c, g = h // HG, h % HG
                    rows = slice(32 * g, 32 * g + 32)
                    for q in range(QT):
                        ins = pe.matmul(bank[:, q * S:(q + 1) * S], q_st[par][rows, c, q * P:(q + 1) * P],
                                        k_hi[par][rows, c, :], start=True, stop=True)
                    ins.then_inc(s_ps, 1)

            def pair_scores(b, par, j):
                wait(pe, prob_ready, b * 8 + j - 1)
                heads = [(e, (2 * j + e) // HG, (2 * j + e) % HG) for e in range(2)]
                for e, c, g in heads:
                    rows = slice(32 * g, 32 * g + 32)
                    pe.matmul(ps_st[j % 2][:, e, :, :], head_row[rows, 2 * j + e, :], spread(m_t[rows, :], 1, QT),
                              start=True, stop=False)
                for kt in range(QT):
                    for k_part in (k_hi, k_lo):
                        for e, c, g in heads:
                            rows = slice(32 * g, 32 * g + 32)
                            ins = pe.matmul(ps_st[j % 2][:, e, kt, :], k_part[par][rows, c, kt * P:(kt + 1) * P],
                                            q_st[par][rows, c, :], start=False, stop=kt == QT - 1 and k_part is k_lo)
                ins.then_inc(st_ps, 1)

            def weigh_values(b, par, j):
                split_wait(pe, b, j)
                if j == 0:
                    pe.wait_ge(v_ready, b + 1)
                if j % 2 == 0:
                    wait(pe, head_out, b * GROUPS + j // 2)
                for h in (2 * j, 2 * j + 1):
                    for kt in range(QT):
                        for p_part, v_part in ((prob_hi, 0), (prob_lo, 0), (prob_hi, 1)):
                            ins = pe.matmul(ps_head[:, 0:S], v[v_part][:, kt, h, :], p_part[j % RING][:, h % 2, kt, :],
                                            start=h % HG == 0 and kt == 0 and p_part is prob_hi and v_part == 0,
                                            stop=h % HG == HG - 1 and kt == QT - 1 and v_part == 1)
                ins.then_inc(pv_done, 1)

            def turn_heads(b, g):
                wait(pe, o_ready, b * GROUPS + g)
                pe.wait_ge(head_out, b * GROUPS + g + 1)
                for q in range(QT):
                    ins = pe.transpose(ps_o[:, g % 2 * QT + q, :, :].rearrange("p h w -> p (h w)"),
                                       head_t[g % 2][:, q * P:(q + 1) * P], ident[:, :])
                ins.then_inc(turned, 1)

            def body(b, par, first=False, last=False):
                pairs = H // 2
                if not last:
                    x_transpose(b + 1)
                max_transpose(b)
                if not first:
                    turn_heads(b - 1, GROUPS - 1)
                if not last:
                    queries(b + 1, 0)
                if not first:
                    o_transpose(b - 1, None if last else b + 1)
                if first:
                    pe.wait_ge(dve_const, 5)
                pe.wait_ge(k_ready, b * 2 + 2)
                pe.wait_ge(mt_ready, b + 1)
                pair_scores(b, par, 0)
                if not last:
                    queries(b + 1, 1, first)
                    keys(b + 1)
                pair_scores(b, par, 1)
                if not first:
                    out_project(b - 1, None if last else b + 1)
                if not last:
                    value_project(b + 1)
                    head_scores(b + 1, 1 - par, 0)
                for j in range(2, pairs):
                    pair_scores(b, par, j)
                    if not last:
                        head_scores(b + 1, 1 - par, j - 1)
                    weigh_values(b, par, j - 2)
                    if j >= 4 and j % 2 == 0:
                        turn_heads(b, (j - 4) // 2)
                if not last:
                    head_scores(b + 1, 1 - par, pairs - 1)
                weigh_values(b, par, pairs - 2)
                turn_heads(b, GROUPS - 2)
                weigh_values(b, par, pairs - 1)

            pe.wait_ge(wq_ready, 1)
            x_transpose(0)
            queries(0, 0)
            queries(0, 1, first=True)
            pe.wait_ge(wk_ready, 1)
            keys(0)
            pe.wait_ge(wv_ready, 1)
            value_project(0)
            for i in range(H // 2):
                head_scores(0, 0, i)
            pe.wait_ge(wo_ready, 1)
            body(0, 0, first=True)
            with pe.Fori(0, B // 2 - 1) as t:
                body(t * 2 + 1, 1)
                body(t * 2 + 2, 0)
            body(B - 1, 1, last=True)
            turn_heads(B - 1, GROUPS - 1)
            o_transpose(B - 1, None)
            out_project(B - 1, None)


def constants_phase(nc, shared, dram):
    with ExitStack() as ctx:
        gates = ctx.enter_context(nc.sbuf_tensor("gates_sb", [P, 4], F32))
        sem = semaphores(nc, ctx)
        g_ld, zeroed, ident_ready, tanh_done = (
            sem(n) for n in ("g_ld", "zeroed", "ident_ready", "tanh_done"))
        block = ctx.enter_context(nc.Block())

        @block.sync
        def _(sp):
            sp.dma_start(gates[:, :], dram["gates"]).then_inc(g_ld, 16)
            sp.wait_ge(zeroed, 2)
            sp.dma_start(dram["xe"].rearrange("(t p) d -> p t d", p=P),
                         spread(shared["zeros"][:, :], 1, L0_BLOCKS * QT)).then_inc(shared["cleared"], 16)
            sp.dma_start(dram["ye"][SLOTS:SLOTS + 1, :], shared["zeros"][0:1, :]).then_inc(shared["cleared"], 16)

        @block.scalar
        def _(act):
            act.wait_ge(g_ld, 16)
            act.activation(shared["tanh_g"][:, :], gates[:, :], ACT.Tanh).then_inc(tanh_done, 1)
            act.wait_ge(tanh_done, 1)

        @block.gpsimd
        def _(pool):
            pool.memset(shared["ident"][:, :], 0.0).then_inc(zeroed, 1)
            pool.memset(shared["zeros"][:, :], 0.0).then_inc(zeroed, 1)
            pool.memset(shared["ones"][:, :], 1.0).then_inc(zeroed, 1)
            pool.wait_ge(zeroed, 3)
            pool.affine_select(out=shared["ident"][:, :], in_=shared["ident"][:, :], compare_op=ALU.not_equal, fill=1.0,
                               base=0, pattern=[[-1, P]], channel_multiplier=1).then_inc(ident_ready, 1)
            pool.affine_select(out=shared["before"][:, :], in_=shared["ones"][:, :], compare_op=ALU.is_gt, fill=0.0,
                               base=0, pattern=[[1, P]], channel_multiplier=-1).then_inc(ident_ready, 1)
            pool.iota(shared["expert_no"][:, :], pattern=[[1, E]], base=0, channel_multiplier=0).then_inc(ident_ready, 1)
            pool.iota(shared["block_no"][:, :], pattern=[[1, L0_BLOCKS]], base=0, channel_multiplier=0).then_inc(ident_ready, 1)
            pool.iota(shared["row_no"][:, :], pattern=[[1, 1]], base=0, channel_multiplier=1).then_inc(ident_ready, 1)
            pool.wait_ge(ident_ready, 5)


def route_phase(nc, layer, shared, dram):
    x, ident = shared["x"], shared["ident"]
    tg = shared["tanh_g"][:, 2 + layer:3 + layer]

    with ExitStack() as ctx:
        def sb(name, shape, dt=F32):
            return ctx.enter_context(nc.sbuf_tensor(f"{name}_r{layer}", shape, dt))

        def ps(name, shape):
            return ctx.enter_context(nc.psum_tensor(f"{name}_r{layer}", shape, F32))

        new_sem = semaphores(nc, ctx)

        def sem(name):
            return new_sem(f"{name}_r{layer}")

        gate_w = sb("gate_w", [P, KC, E])
        gate_b = sb("gate_b", [P, E])
        xn = sb("xn", [P, TT, D])
        stats, mean_var = sb("stats", [P, TT, 6]), sb("mean_var", [P, TT, 2])
        var_eps, rstd, minus_half = sb("var_eps", [P, TT]), sb("rstd", [P, TT]), sb("minus_half", [P, TT])
        xt = [sb(f"xt{i}", [P, KC, P]) for i in range(2)]
        exp_no, exp_rank, blk_no, row_no = sb("exp_no", [P, E]), sb("exp_rank", [P, E]), sb("blk_no", [P, L0_BLOCKS]), sb("row_no", [P, 1])
        score, score2, tmp = sb("score", [P, TT, E]), sb("score2", [P, TT, E]), sb("tmp", [P, TT, E])
        shifted, expo = sb("shifted", [P, TT, E]), sb("expo", [P, TT, E])
        top = [sb(f"top{i}", [P, TT]) for i in range(2)]
        col = [sb(f"col{i}", [P, TT]) for i in range(2)]
        one_hot = [sb(f"one_hot{i}", [P, TT, E]) for i in range(2)]
        chosen = sb("chosen", [P, TT, E], BF16)
        wt = [sb(f"wt{i}", [P, TT]) for i in range(2)]
        diff, ratio, den = sb("diff", [P, TT]), sb("ratio", [P, TT]), sb("den", [P, TT])
        count, blocks_i, blocks_f = sb("count", [P, E], I32), sb("blocks_i", [P, E], I32), sb("blocks_f", [P, E])
        earlier, first, end = sb("earlier", [P, E, E]), sb("first", [P, E]), sb("end", [P, E])
        base, place, valid = sb("base", [P, E]), sb("place", [P, TT, E]), sb("valid", [P, TT, E])
        past, blk_expert = sb("past", [P, L0_BLOCKS, E]), sb("blk_expert", [P, L0_BLOCKS])
        noop = [sb(f"noop{i}", [P, TT]) for i in range(2)]

        ps_xt = [ps(f"ps_xt{i}", [P, KC, P]) for i in range(2)]
        ps_lg = ps("ps_lg", [P, TT, E])
        ps_rank = ps("ps_rank", [P, TT, E])
        ps_cnt = ps("ps_cnt", [P, E])

        g_ld, const, ln_stats, ln_mean, ln_eps, ln_rstd, xn_ready, xt_ps, xt_ready, lg_ps = (
            sem(n) for n in ("g_ld", "const", "ln_stats", "ln_mean", "ln_eps", "ln_rstd", "xn_ready", "xt_ps",
                             "xt_ready", "lg_ps"))
        step, exp_in, exp_done, chosen_ready, rank_ps, slots_ready, scattered = (
            sem(n) for n in ("step", "exp_in", "exp_done", "chosen_ready", "rank_ps", "slots_ready", "scattered"))
        block = ctx.enter_context(nc.Block())

        @block.sync
        def _(sp):
            sp.dma_start(gate_w[:, :, :], dram["gate_w"].rearrange("(k p) e -> p k e", p=P)).then_inc(g_ld, 16)
            if layer:
                sp.dma_start(gate_b[:, :], dram["gate_b"]).then_inc(g_ld, 16)

        @block.gpsimd
        def _(pool):
            pool.memset(minus_half[:, :], -0.5).then_inc(const, 1)
            pool.wait_ge(const, 1)
            for c in range(TT // CT):
                tiles = slice(c * CT, c * CT + CT)
                pool.wait_ge(ln_mean, c * CT + CT)
                pool.tensor_scalar(var_eps[:, tiles], mean_var[:, tiles, 1], EPS, None, ALU.add).then_inc(ln_eps, 1)
                pool.wait_ge(ln_eps, c + 1)
                pool.tensor_tensor(rstd[:, tiles], var_eps[:, tiles], minus_half[:, tiles], ALU.pow).then_inc(ln_rstd, 1)
            pool.wait_ge(slots_ready, 2)
            pool.wait_ge(shared["cleared"], 32)
            for i in range(2):
                for t in range(TT):
                    pool.indirect_dma_start(
                        out=dram["xe"], out_offset=bass.IndirectOffsetOnAxis(ap=shared["slot"][i][:, t:t + 1], axis=0),
                        in_=xn[:, t, :], in_offset=None, bounds_check=SLOTS - 1,
                        oob_is_err=False).then_inc(scattered, 16)
            pool.wait_ge(scattered, 16 * 2 * TT)

        @block.scalar
        def _(act):
            with act.Fori(0, TT // 2) as t:
                for i in range(2):
                    act.wait_ge(xt_ps, t * 2 + i + 1)
                    act.activation(xt[i][:, :, :], ps_xt[i][:, :, :], ACT.Copy).then_inc(xt_ready, 1)
            act.wait_ge(exp_in, 1)
            if layer == 0:
                act.activation(ratio[:, :], diff[:, :], ACT.Exp).then_inc(exp_done, 1)
            else:
                act.activation(expo[:, :, :], shifted[:, :, :], ACT.Exp).then_inc(exp_done, 1)

        @block.tensor
        def _(pe):
            def turn(t, i):
                pe.wait_ge(xn_ready, t + 1)
                for k in range(KC):
                    ins = pe.transpose(ps_xt[i][:, k, :], xn[:, t, k * P:(k + 1) * P], ident[:, :])
                ins.then_inc(xt_ps, 1)

            def logits(t, i):
                pe.wait_ge(xt_ready, t + 1)
                for k in range(KC):
                    ins = pe.matmul(ps_lg[:, t, :], xt[i][:, k, :], gate_w[:, k, :],
                                    start=k == 0, stop=k == KC - 1)
                ins.then_inc(lg_ps, 1)

            pe.wait_ge(g_ld, 16 + 16 * layer)
            turn(0, 0)
            for t in range(1, TT):
                turn(t, t % 2)
                logits(t - 1, 1 - t % 2)
            logits(TT - 1, (TT - 1) % 2)
            pe.wait_ge(chosen_ready, 1)
            pe.matmul(ps_rank[:, :, :], shared["before"][:, :], chosen[:, :, :], start=True, stop=False)
            for s in range(TT - 1):
                pe.matmul(ps_rank[:, s + 1:TT, :], shared["ones"][:, :], spread(chosen[:, s, :], 1, TT - 1 - s),
                          start=False, stop=s == TT - 2)
            for s in range(TT):
                ins = pe.matmul(ps_cnt[:, :], shared["ones"][:, :], chosen[:, s, :], start=s == 0, stop=s == TT - 1)
            ins.then_inc(rank_ps, 1)

        @block.vector
        def _(dve):
            n = 0

            dve.tensor_copy(exp_no[:, :], shared["expert_no"][:, :]).then_inc(const, 1)
            dve.tensor_copy(blk_no[:, :], shared["block_no"][:, :]).then_inc(const, 1)
            dve.tensor_copy(row_no[:, :], shared["row_no"][:, :]).then_inc(const, 1)
            dve.wait_ge(const, 4)
            dve.tensor_scalar(exp_rank[:, :], exp_no[:, :], -1.0, float(E), ALU.mult, ALU.add).then_inc(const, 1)
            dve.tensor_tensor(earlier[:, :, :], spread(exp_no[:, :], 1, E), spread(exp_no[:, :], 2, E),
                              ALU.is_lt).then_inc(const, 1)
            dve.wait_ge(const, 6)

            def moments(c):
                for t in range(c * CT, c * CT + CT):
                    dve.bn_stats(stats[:, t, :], x[:, t, :]).then_inc(ln_stats, 1)
                for t in range(c * CT, c * CT + CT):
                    dve.wait_ge(ln_stats, t + 1)
                    dve.bn_aggr(mean_var[:, t, :], stats[:, t, :]).then_inc(ln_mean, 1)

            def normalise(c):
                dve.wait_ge(ln_rstd, c + 1)
                for t in range(c * CT, c * CT + CT):
                    dve.tensor_scalar(xn[:, t, :], x[:, t, :], mean_var[:, t, 0:1], rstd[:, t:t + 1], ALU.subtract,
                                      ALU.mult).then_inc(xn_ready, 1)

            moments(0)
            for c in range(1, TT // CT):
                moments(c)
                normalise(c - 1)
            normalise(TT // CT - 1)

            dve.wait_ge(lg_ps, TT)
            if layer == 0:
                dve.tensor_copy(score[:, :, :], ps_lg[:, :, :]).then_inc(step, 1)
                dve.wait_ge(step, 1)
            else:
                dve.wait_ge(g_ld, 32)
                dve.tensor_tensor(tmp[:, :, :], ps_lg[:, :, :], spread(gate_b[:, :], 1, TT), ALU.add).then_inc(step, 1)
                dve.wait_ge(step, 1)
                dve.tensor_reduce(den[:, :], tmp[:, :, :], AX.X, ALU.max).then_inc(step, 1)
                dve.wait_ge(step, 2)
                dve.tensor_tensor(shifted[:, :, :], tmp[:, :, :], spread(den[:, :], 2, E), ALU.subtract).then_inc(exp_in, 1)
                dve.wait_ge(exp_done, 1)
                dve.tensor_reduce(diff[:, :], expo[:, :, :], AX.X, ALU.add).then_inc(step, 1)
                dve.wait_ge(step, 3)
                dve.reciprocal(ratio[:, :], diff[:, :]).then_inc(step, 1)
                dve.wait_ge(step, 4)
                dve.tensor_tensor(score[:, :, :], expo[:, :, :], spread(ratio[:, :], 2, E), ALU.mult).then_inc(step, 1)
                dve.wait_ge(step, 5)
            n = 5 if layer else 1

            for i in range(2):
                src = score2 if i else score
                if i:
                    dve.scalar_tensor_tensor(score2[:, :, :], one_hot[0][:, :, :], -3e38, score[:, :, :], ALU.mult,
                                             ALU.add).then_inc(step, 1)
                    dve.wait_ge(step, n + 5)
                m = n + 5 * i
                dve.tensor_reduce(top[i][:, :], src[:, :, :], AX.X, ALU.max).then_inc(step, 1)
                dve.wait_ge(step, m + 1)
                dve.tensor_tensor(tmp[:, :, :], src[:, :, :], spread(top[i][:, :], 2, E), ALU.is_equal).then_inc(step, 1)
                dve.wait_ge(step, m + 2)
                dve.tensor_tensor(valid[:, :, :], tmp[:, :, :], spread(exp_rank[:, :], 1, TT), ALU.mult).then_inc(step, 1)
                dve.wait_ge(step, m + 3)
                dve.tensor_reduce(col[i][:, :], valid[:, :, :], AX.X, ALU.max).then_inc(step, 1)
                dve.wait_ge(step, m + 4)
                dve.tensor_tensor(one_hot[i][:, :, :], spread(exp_rank[:, :], 1, TT), spread(col[i][:, :], 2, E),
                                  ALU.is_equal).then_inc(step, 1)
                if i == 0:
                    dve.wait_ge(step, m + 5)
                    n += 1
            n += 10
            dve.wait_ge(step, n)

            if layer == 1:
                for i in range(2):
                    dve.tensor_scalar(col[i][:, :], top[i][:, :], 0.0, None, ALU.is_gt).then_inc(step, 1)
                    dve.wait_ge(step, n + 2 * i + 1)
                    dve.tensor_tensor(one_hot[i][:, :, :], one_hot[i][:, :, :], spread(col[i][:, :], 2, E),
                                      ALU.mult).then_inc(step, 1)
                    dve.wait_ge(step, n + 2 * i + 2)
                n += 4
            dve.tensor_tensor(chosen[:, :, :], one_hot[0][:, :, :], one_hot[1][:, :, :], ALU.add).then_inc(chosen_ready, 1)

            if layer == 0:
                dve.tensor_tensor(diff[:, :], top[1][:, :], top[0][:, :], ALU.subtract).then_inc(exp_in, 1)
                dve.wait_ge(exp_done, 1)
                dve.tensor_scalar(den[:, :], ratio[:, :], 1.0, None, ALU.add).then_inc(step, 1)
                dve.wait_ge(step, n + 1)
                dve.reciprocal(wt[0][:, :], den[:, :]).then_inc(step, 1)
                dve.wait_ge(step, n + 2)
                dve.tensor_tensor(wt[1][:, :], ratio[:, :], wt[0][:, :], ALU.mult).then_inc(step, 1)
                dve.wait_ge(step, n + 3)
                n += 3
            weights = top if layer else wt
            for i in range(2):
                dve.tensor_scalar(shared["weight"][i][:, :], weights[i][:, :], tg, None, ALU.mult).then_inc(step, 1)
            n += 2
            dve.wait_ge(step, n)

            dve.wait_ge(rank_ps, 1)
            if layer == 0:
                dve.tensor_scalar(count[:, :], ps_cnt[:, :], float(SB - 1), None, ALU.add).then_inc(step, 1)
                dve.wait_ge(step, n + 1)
                dve.tensor_scalar(blocks_i[:, :], count[:, :], SB.bit_length() - 1, None,
                                  ALU.arith_shift_right).then_inc(step, 1)
                dve.wait_ge(step, n + 2)
                dve.tensor_copy(blocks_f[:, :], blocks_i[:, :]).then_inc(step, 1)
                dve.wait_ge(step, n + 3)
                dve.tensor_tensor(earlier[:, :, :], earlier[:, :, :], spread(blocks_f[:, :], 1, E), ALU.mult).then_inc(step, 1)
                dve.wait_ge(step, n + 4)
                dve.tensor_reduce(first[:, :], earlier[:, :, :], AX.X, ALU.add).then_inc(step, 1)
                dve.wait_ge(step, n + 5)
                dve.tensor_scalar(base[:, :], first[:, :], float(SB), float(-SLOTS), ALU.mult, ALU.add).then_inc(step, 1)
                dve.tensor_tensor(end[:, :], first[:, :], blocks_f[:, :], ALU.add).then_inc(step, 1)
                dve.wait_ge(step, n + 7)
                n += 7
                dve.tensor_tensor(place[:, :, :], ps_rank[:, :, :], spread(base[:, :], 1, TT), ALU.add).then_inc(step, 1)
                dve.tensor_tensor(past[:, :, :], spread(end[:, :], 1, L0_BLOCKS), spread(blk_no[:, :], 2, E),
                                  ALU.is_le).then_inc(step, 1)
                dve.wait_ge(step, n + 2)
                dve.tensor_reduce(blk_expert[:, :], past[:, :, :], AX.X, ALU.add).then_inc(step, 1)
                dve.wait_ge(step, n + 3)
                dve.tensor_scalar(shared["block_expert"][:, :], blk_expert[:, :], float(E - 1), None,
                                  ALU.min).then_inc(step, 1)
                dve.tensor_scalar(blk_expert[:, :], blk_expert[:, :], float(E - 1), float(P), ALU.min, ALU.mult).then_inc(step, 1)
                dve.wait_ge(step, n + 5)
                dve.tensor_scalar(shared["block_row"][:, :], blk_expert[:, :], row_no[:, 0:1], None, ALU.add).then_inc(step, 1)
                n += 6
            else:
                dve.tensor_scalar(base[:, :], exp_no[:, :], float(SB), float(-SLOTS), ALU.mult, ALU.add).then_inc(step, 1)
                dve.tensor_scalar(valid[:, :, :], ps_rank[:, :, :], float(SB), None, ALU.is_lt).then_inc(step, 1)
                dve.tensor_scalar(first[:, :], exp_no[:, :], float(E - 1), None, ALU.is_lt).then_inc(step, 1)
                dve.wait_ge(step, n + 3)
                dve.tensor_tensor(tmp[:, :, :], ps_rank[:, :, :], spread(base[:, :], 1, TT), ALU.add).then_inc(step, 1)
                dve.tensor_tensor(valid[:, :, :], valid[:, :, :], spread(first[:, :], 1, TT), ALU.mult).then_inc(step, 1)
                dve.wait_ge(step, n + 5)
                dve.tensor_tensor(place[:, :, :], tmp[:, :, :], valid[:, :, :], ALU.mult).then_inc(step, 1)
                n += 6
            dve.wait_ge(step, n)
            for i in range(2):
                dve.tensor_tensor(tmp[:, :, :], one_hot[i][:, :, :], place[:, :, :], ALU.mult).then_inc(step, 1)
                dve.wait_ge(step, n + 3 * i + 1)
                dve.tensor_reduce(col[i][:, :], tmp[:, :, :], AX.X, ALU.add).then_inc(step, 1)
                dve.wait_ge(step, n + 3 * i + 2)
                dve.tensor_scalar(shared["slot"][i][:, :], col[i][:, :], float(SLOTS), None, ALU.add).then_inc(slots_ready, 1)
                if i == 0:
                    dve.sem_inc(step, 1)
            n += 5

            if layer == 1:
                for i in range(2):
                    dve.tensor_tensor(noop[i][:, :], one_hot[i][:, :, E - 1], shared["weight"][i][:, :], ALU.mult).then_inc(step, 1)
                dve.wait_ge(step, n + 2)
                dve.tensor_tensor(noop[0][:, :], noop[0][:, :], noop[1][:, :], ALU.add).then_inc(step, 1)
                dve.wait_ge(step, n + 3)
                for t in range(TT):
                    dve.scalar_tensor_tensor(x[:, t, :], xn[:, t, :], noop[0][:, t:t + 1], x[:, t, :], ALU.mult,
                                             ALU.add).then_inc(step, 1)
                n += 3 + TT
            dve.wait_ge(step, n)
            dve.wait_ge(slots_ready, 2)


def expert_phase(nc, layer, shared, dram):
    ident = shared["ident"]
    blocks = E - 1 if layer else L0_BLOCKS
    RB = 4

    with ExitStack() as ctx:
        def sb(name, shape, dt=F32):
            return ctx.enter_context(nc.sbuf_tensor(f"{name}_e{layer}", shape, dt))

        def ps(name, shape):
            return ctx.enter_context(nc.psum_tensor(f"{name}_e{layer}", shape, F32))

        new_sem = semaphores(nc, ctx)

        def sem(name):
            return new_sem(f"{name}_e{layer}")

        w1_raw = [sb(f"w1_raw{i}", [P, KC * F]) for i in range(2)]
        w2_raw = [sb(f"w2_raw{i}", [P, FC * D]) for i in range(2)]
        w1 = [[sb(f"w1_{i}{j}", [P, KC, FC, P], F32R) for j in range(2)] for i in range(2)]
        w2 = [[sb(f"w2_{i}{j}", [P, FC, D], F32R) for j in range(2)] for i in range(2)]
        b1 = [sb(f"b1_{i}", [P, FC]) for i in range(2)]
        b2 = [sb(f"b2_{i}", [P, D]) for i in range(2)]
        xe = [sb(f"xe{i}", [P, QT, D]) for i in range(2)]
        xe_t = [[sb(f"xe_t{i}{j}", [P, KC, SB], F32R) for j in range(2)] for i in range(2)]
        hid = [sb(f"hid{i}", [P, 2, SB]) for i in range(2)]
        h = [[sb(f"h{i}{j}", [P, FC, SB], F32R) for j in range(2)] for i in range(2)]
        y = [sb(f"y{i}", [P, QT, D]) for i in range(2)]

        ps_x = [ps(f"ps_x{i}", [P, KC, SB]) for i in range(2)]
        ps_h = [ps(f"ps_h{i}", [P, 2, SB]) for i in range(RB)]
        ps_y = [ps(f"ps_y{i}", [P, QT, D]) for i in range(2)]

        w1_ld, w2_ld, b1_ld, b2_ld, xe_ld, stored = (
            [sem(f"{n}{i}") for i in range(2)] for n in ("w1_ld", "w2_ld", "b1_ld", "b2_ld", "xe_ld", "stored"))
        w1_hi, w1_ready, w2_hi, w2_ready, xe_ps, xe_hi, xe_ready, h_ps, hid_ready, h_hi, h_ready, y_ps, y_ready = (
            sem(n) for n in ("w1_hi", "w1_ready", "w2_hi", "w2_ready", "xe_ps", "xe_hi", "xe_ready", "h_ps",
                             "hid_ready", "h_hi", "h_ready", "y_ps", "y_ready"))
        loaded = {"w1": w1_ld, "w2": w2_ld, "b1": b1_ld, "b2": b2_ld}
        indexed = {n: sem(f"{n}_indexed") for n in loaded}
        index = {n: [sb(f"{n}_index{i}", [P, 1], I32) for i in range(2)] for n in loaded}
        passed = sem("passed")
        NP = FC // 2

        block = ctx.enter_context(nc.Block())
        xe_src = dram["xe"].rearrange("(b q p) d -> p b q d", p=P, q=QT)
        ye_dst = dram["ye"][0:SLOTS, :].rearrange("(b q p) d -> p b q d", p=P, q=QT)

        def one(ap, b):
            return ap[:, bass.ds(b, 1), :, :].rearrange("p b q d -> p (b q) d")

        def load_rows(pool, kind, dst, numbers, b, i):
            if layer:
                pool.dma_start(dst[:, :], dram[kind][bass.ds(b * P, P), :]).then_inc(loaded[kind][i], 16)
            else:
                pool.tensor_copy(index[kind][i][:, :], shared[numbers][:, bass.ds(b, 1)]).then_inc(indexed[kind], 1)
                wait_apart(pool, indexed[kind], b + 1, passed)
                pool.indirect_dma_start(
                    out=dst[:, :], out_offset=None, in_=dram[kind],
                    in_offset=bass.IndirectOffsetOnAxis(ap=index[kind][i][:, :], axis=0)).then_inc(loaded[kind][i], 16)

        @block.sync
        def _(sp):
            def load_x(b, i):
                sp.dma_start(xe[i][:, :, :], one(xe_src, b)).then_inc(xe_ld[i], 16)

            def store(b, i):
                sp.wait_ge(y_ready, b + 1)
                sp.dma_start(one(ye_dst, b), y[i][:, :, :]).then_inc(stored[i], 16)

            load_x(0, 0)
            load_x(1, 1)
            with sp.Fori(0, (blocks - 2) // 2) as t:
                for i in range(2):
                    sp.wait_ge(xe_ps, t * 2 + i + 1)
                    load_x(t * 2 + i + 2, i)
                    store(t * 2 + i, i)
            for b in range((blocks - 2) // 2 * 2, blocks):
                if b + 2 < blocks:
                    sp.wait_ge(xe_ps, b + 1)
                    load_x(b + 2, b % 2)
                store(b, b % 2)
            for i in range(2):
                sp.wait_ge(stored[i], 16 * ((blocks - i + 1) // 2))

        @block.gpsimd
        def _(pool):
            def load_w1(b, i):
                load_rows(pool, "w1", w1_raw[i], "block_row", b, i)

            def load_w2(b, i):
                load_rows(pool, "w2", w2_raw[i], "block_row", b, i)

            def load_b1(b, i):
                if layer == 0:
                    load_rows(pool, "b1", b1[i], "block_row", b, i)

            def load_b2(b, i):
                if layer == 0:
                    load_rows(pool, "b2", b2[i], "block_expert", b, i)

            def body(b, i, first=False, w1_more=True, w2_more=True):
                if w1_more:
                    wait_apart(pool, w1_ready, b + 1, passed)
                    load_w1(b + 2, i)
                if w2_more:
                    if not first:
                        wait_apart(pool, w2_ready, b, passed)
                    load_w2(b + 1, 1 - i)
                if layer == 0:
                    if w1_more:
                        wait_apart(pool, hid_ready, (b + 1) * NP, passed)
                        load_b1(b + 2, i)
                    if w2_more:
                        if not first:
                            wait_apart(pool, y_ready, b, passed)
                        load_b2(b + 1, 1 - i)

            load_w1(0, 0)
            load_w2(0, 0)
            load_w1(1, 1)
            load_b1(0, 0)
            load_b1(1, 1)
            load_b2(0, 0)
            body(0, 0, first=True)
            with pool.Fori(0, (blocks - 3) // 2) as t:
                body(t * 2 + 1, 1)
                body(t * 2 + 2, 0)
            for b in range((blocks - 3) // 2 * 2 + 1, blocks):
                body(b, b % 2, w1_more=b + 2 < blocks, w2_more=b + 1 < blocks)

        def w1_view(raw, k):
            return raw[:, k * F:(k + 1) * F].rearrange("p (f j) -> p j f", j=FC)

        @block.scalar
        def _(act):
            def w1_high(b, i, half, k):
                if k == 0:
                    act.wait_ge(w1_ld[i], (half + 1) * 16)
                    wait(act, h_ps, (b - 1) * NP)
                act.activation(w1[i][0][:, k, :, :], w1_view(w1_raw[i], k), ACT.Copy).then_inc(w1_hi, 1)

            def w2_high(b, i, half, k):
                if k == 0:
                    act.wait_ge(w2_ld[i], (half + 1) * 16)
                    wait(act, y_ps, b - 1)
                js = slice(k * FC // 2, (k + 1) * FC // 2)
                act.activation(w2[i][0][:, js, :], w2_raw[i][:, :].rearrange("p (j d) -> p j d", d=D)[:, js, :],
                               ACT.Copy).then_inc(w2_hi, 1)

            def hidden(b, i, half, jp):
                act.wait_ge(h_ps, b * NP + jp + 1)
                wait(act, h_ready, b * NP + jp - 1)
                if layer:
                    act.activation(hid[jp % 2][:, :, :], ps_h[jp % RB][:, :, :], ACT.Relu).then_inc(hid_ready, 1)
                else:
                    if jp == 0:
                        act.wait_ge(b1_ld[i], (half + 1) * 16)
                    for j in range(2):
                        ins = act.activation(hid[jp % 2][:, j, :], ps_h[jp % RB][:, j, :], ACT.Gelu,
                                             bias=b1[i][:, 2 * jp + j:2 * jp + j + 1])
                    ins.then_inc(hid_ready, 1)

            def body(b, i, half, more=True):
                act.wait_ge(xe_ps, b + 1)
                act.activation(xe_t[i][0][:, :, :], ps_x[i][:, :, :], ACT.Copy).then_inc(xe_hi, 1)
                for jp in range(NP):
                    if jp < KC:
                        if more:
                            w1_high(b + 1, 1 - i, half + i, jp)
                    else:
                        w2_high(b, i, half, jp - KC)
                    hidden(b, i, half, jp)

            for k in range(KC):
                w1_high(0, 0, 0, k)
            body(0, 0, 0)
            with act.Fori(0, (blocks - 2) // 2) as t:
                body(t * 2 + 1, 1, t)
                body(t * 2 + 2, 0, t + 1)
            for b in range((blocks - 2) // 2 * 2 + 1, blocks):
                body(b, b % 2, b // 2, more=b + 1 < blocks)

        @block.vector
        def _(dve):
            def w1_low(b, i, k):
                dve.wait_ge(w1_hi, b * KC + k + 1)
                ins = dve.tensor_tensor(w1[i][1][:, k, :, :], w1_view(w1_raw[i], k), w1[i][0][:, k, :, :].bitcast(F32),
                                        ALU.subtract)
                if k == KC - 1:
                    ins.then_inc(w1_ready, 1)

            def w2_low(b, i, k):
                dve.wait_ge(w2_hi, b * 2 + k + 1)
                js = slice(k * FC // 2, (k + 1) * FC // 2)
                ins = dve.tensor_tensor(w2[i][1][:, js, :], w2_raw[i][:, :].rearrange("p (j d) -> p j d", d=D)[:, js, :],
                                        w2[i][0][:, js, :].bitcast(F32), ALU.subtract)
                if k == 1:
                    ins.then_inc(w2_ready, 1)

            def hidden_parts(b, i, jp):
                js = slice(2 * jp, 2 * jp + 2)
                dve.wait_ge(hid_ready, b * NP + jp + 1)
                wait(dve, y_ps, b - 1)
                dve.tensor_copy(h[i][0][:, js, :], hid[jp % 2][:, :, :]).then_inc(h_hi, 1)
                dve.wait_ge(h_hi, b * NP + jp + 1)
                dve.tensor_tensor(h[i][1][:, js, :], hid[jp % 2][:, :, :], h[i][0][:, js, :].bitcast(F32),
                                  ALU.subtract).then_inc(h_ready, 1)

            def output(b, i, half):
                dve.wait_ge(y_ps, b + 1)
                wait(dve, stored[i], half * 16)
                if layer:
                    dve.tensor_copy(y[i][:, :, :], ps_y[i][:, :, :]).then_inc(y_ready, 1)
                else:
                    dve.wait_ge(b2_ld[i], (half + 1) * 16)
                    dve.tensor_tensor(y[i][:, :, :], ps_y[i][:, :, :], spread(b2[i][:, :], 1, QT), ALU.add).then_inc(y_ready, 1)

            def body(b, i, half, first=False, more=True):
                dve.wait_ge(xe_hi, b + 1)
                dve.tensor_tensor(xe_t[i][1][:, :, :], ps_x[i][:, :, :], xe_t[i][0][:, :, :].bitcast(F32),
                                  ALU.subtract).then_inc(xe_ready, 1)
                for jp in range(NP):
                    if jp < KC:
                        if more:
                            w1_low(b + 1, 1 - i, jp)
                    else:
                        w2_low(b, i, jp - KC)
                    hidden_parts(b, i, jp)
                if not first:
                    output(b - 1, 1 - i, half - 1 + i)

            for k in range(KC):
                w1_low(0, 0, k)
            body(0, 0, 0, first=True)
            with dve.Fori(0, (blocks - 2) // 2) as t:
                body(t * 2 + 1, 1, t)
                body(t * 2 + 2, 0, t + 1)
            for b in range((blocks - 2) // 2 * 2 + 1, blocks):
                body(b, b % 2, b // 2, more=b + 1 < blocks)
            output(blocks - 1, (blocks - 1) % 2, (blocks - 1) // 2)

        @block.tensor
        def _(pe):
            def turn(b, i, half):
                pe.wait_ge(xe_ld[i], (half + 1) * 16)
                wait(pe, xe_ready, b - 1)
                for q in range(QT):
                    rows = xe[i][:, q, :].rearrange("p (d k) -> p k d", k=KC)
                    for k in range(KC):
                        ins = pe.transpose(ps_x[i][:, k, q * P:(q + 1) * P], rows[:, k, :], ident[:, :])
                ins.then_inc(xe_ps, 1)

            def first_product(b, i, more, half):
                pe.wait_ge(xe_ready, b + 1)
                pe.wait_ge(w1_ready, b + 1)
                for jp in range(NP):
                    wait(pe, hid_ready, b * NP + jp + 1 - RB)
                    for j in range(2):
                        for k in range(KC):
                            ins = split_matmul(pe, ps_h[jp % RB][:, j, :], [w1[i][s][:, k, 2 * jp + j, :] for s in range(2)],
                                               [xe_t[i][s][:, k, :] for s in range(2)], k == 0, k == KC - 1)
                    ins.then_inc(h_ps, 1)
                    if jp == NP - 2 and more:
                        turn(b + 1, 1 - i, half + i)

            def second_product(b, i):
                pe.wait_ge(w2_ready, b + 1)
                pe.wait_ge(h_ready, (b + 1) * NP)
                wait(pe, y_ready, b - 1)
                for q in range(QT):
                    for j in range(FC):
                        ins = split_matmul(pe, ps_y[i][:, q, :], [h[i][s][:, j, q * P:(q + 1) * P] for s in range(2)],
                                           [w2[i][s][:, j, :] for s in range(2)], j == 0, j == FC - 1)
                ins.then_inc(y_ps, 1)

            def body(b, i, half, more=True):
                first_product(b, i, more, half)
                second_product(b - 1, 1 - i)

            turn(0, 0, 0)
            first_product(0, 0, True, 0)
            body(1, 1, 0)
            with pe.Fori(1, blocks // 2) as t:
                body(t * 2, 0, t)
                body(t * 2 + 1, 1, t)
            for b in range(blocks // 2 * 2, blocks):
                body(b, b % 2, b // 2, more=b + 1 < blocks)
            second_product(blocks - 1, (blocks - 1) % 2)


def combine_phase(nc, layer, shared, dram):
    x = shared["x"]
    RY = 4
    with ExitStack() as ctx:
        rows = [[ctx.enter_context(nc.sbuf_tensor(f"rows{r}{i}_c{layer}", [P, D], F32)) for i in range(2)] for r in range(RY)]
        sem = semaphores(nc, ctx)
        rows_ld = [sem(f"rows_ld{r}_c{layer}") for r in range(RY)]
        added = sem(f"added_c{layer}")
        half_added = sem(f"half_added_c{layer}")
        stored = sem(f"out_stored_c{layer}")
        block = ctx.enter_context(nc.Block())

        @block.gpsimd
        def _(pool):
            def gather(t, r):
                for i in range(2):
                    pool.indirect_dma_start(
                        out=rows[r][i][:, :], out_offset=None, in_=dram["ye"],
                        in_offset=bass.IndirectOffsetOnAxis(ap=shared["slot"][i][:, t:t + 1], axis=0)).then_inc(rows_ld[r], 16)

            for t in range(TT):
                wait(pool, added, t - RY + 1)
                gather(t, t % RY)

        @block.vector
        def _(dve):
            with dve.Fori(0, TT // RY) as u:
                for r in range(RY):
                    xt = x[:, bass.ds(u * RY + r, 1), :].rearrange("p t d -> p (t d)")
                    dve.wait_ge(rows_ld[r], (u + 1) * 32)
                    dve.scalar_tensor_tensor(xt, rows[r][0][:, :], shared["weight"][0][:, bass.ds(u * RY + r, 1)], xt,
                                             ALU.mult, ALU.add).then_inc(half_added, 1)
                    dve.wait_ge(half_added, u * RY + r + 1)
                    dve.scalar_tensor_tensor(xt, rows[r][1][:, :], shared["weight"][1][:, bass.ds(u * RY + r, 1)], xt,
                                             ALU.mult, ALU.add).then_inc(added, 1)
            dve.wait_ge(added, TT)

        if layer == LAYERS[-1]:
            @block.sync
            def _(sp):
                dst = dram["out"].rearrange("(t p) d -> p t d", p=P)
                for u in range(TT // RY):
                    tiles = slice(u * RY, u * RY + RY)
                    sp.wait_ge(added, (u + 1) * RY)
                    sp.dma_start(dst[:, tiles, :], x[:, tiles, :]).then_inc(stored, 16)
                sp.wait_ge(stored, 16 * (TT // RY))


def program(nc, dram):
    with ExitStack() as ctx:
        def sb(name, shape, dt=F32):
            return ctx.enter_context(nc.sbuf_tensor(name, shape, dt))

        shared = {
            "x": sb("x_sb", [P, TT, D]),
            "ident": sb("ident", [P, P]),
            "zeros": sb("zeros", [P, D]),
            "ones": sb("ones", [P, P], BF16),
            "before": sb("before", [P, P], BF16),
            "expert_no": sb("expert_no", [P, E], I32),
            "block_no": sb("block_no", [P, L0_BLOCKS], I32),
            "row_no": sb("row_no_i", [P, 1], I32),
            "tanh_g": sb("tanh_g", [P, 4]),
            "slot": [sb(f"slot{i}", [P, TT], I32) for i in range(2)],
            "weight": [sb(f"weight{i}", [P, TT]) for i in range(2)],
            "block_row": sb("block_row", [P, L0_BLOCKS], I32),
            "block_expert": sb("block_expert", [P, L0_BLOCKS], I32),
            "cleared": ctx.enter_context(nc.semaphore("cleared")),
        }
        constants_phase(nc, shared, dram)
        for layer in LAYERS:
            mine = {**dram, **{k[3:]: v for k, v in dram.items() if k.startswith(f"L{layer}_")}}
            attention_phase(nc, layer, shared, mine, layer == 0)
            route_phase(nc, layer, shared, mine)
            expert_phase(nc, layer, shared, mine)
            combine_phase(nc, layer, shared, mine)


def kernel(**inputs):
    import numpy as np
    import concourse.bacc as bacc
    from concourse import mybir as mb
    from concourse.bass_utils import run_bass_kernel_spmd

    nc = bacc.Bacc("TRN2", target_bir_lowering=False, num_devices=1)

    def rows(a):
        return np.broadcast_to(a.reshape(1, -1), (P, a.size))

    def heads_column(bias):
        a = bias.reshape(CH, HG, 1, HD)
        return np.broadcast_to(a, (CH, HG, 2, HD)).reshape(CH, P).T

    a = {"x": inputs["x"].reshape(N, D), "ctx_t": inputs["ctx_1024"].reshape(N, D).T,
         "gates": rows(np.concatenate([inputs["g_xattn"], inputs["g_ffn"]]))}
    for l in ("L0", "L1"):
        for n in "qkvo":
            a[f"{l}_w{n}"] = inputs[f"{l}_xattn_W{n}"].T
        for n in "qk":
            a[f"{l}_b{n}"] = heads_column(inputs[f"{l}_xattn_b{n}"])
        for n in "vo":
            a[f"{l}_b{n}"] = rows(inputs[f"{l}_xattn_b{n}"])
    a["L0_w1"] = inputs["L0_ffn_W1"].reshape(-1, KC * F)
    a["L0_w2"] = inputs["L0_ffn_W2"].reshape(-1, FC * D)
    a["L0_b1"] = inputs["L0_ffn_b1"].reshape(-1, FC)
    a["L0_b2"] = inputs["L0_ffn_b2"]
    a["L1_w1"] = inputs["L1_ffn_experts_inter"].reshape(-1, KC * F)
    a["L1_w2"] = inputs["L1_ffn_experts_out"].reshape(-1, FC * D)
    a["L0_gate_w"] = inputs["L0_ffn_gate_w"]
    a["L1_gate_w"] = inputs["L1_ffn_router_w"].T
    a["L1_gate_b"] = rows(inputs["L1_ffn_router_b"])
    arrays = {k: np.ascontiguousarray(v) for k, v in a.items()}
    dram = {k: nc.dram_tensor(k, v.shape, mb.dt.from_np(v.dtype), kind="ExternalInput").ap() for k, v in arrays.items()}
    dram["xe"] = nc.dram_tensor("expert_rows", (SLOTS, D), F32, kind="Internal").ap()
    dram["ye"] = nc.dram_tensor("expert_out", (SLOTS + 1, D), F32, kind="Internal").ap()
    dram["out"] = nc.dram_tensor("out", (N, D), F32, kind="ExternalOutput").ap()
    program(nc, dram)
    result = run_bass_kernel_spmd(nc, [arrays], core_ids=[0])
    return result.results[0]["out"].reshape(B, S, D)
```

```python
from contextlib import ExitStack

import concourse.bass as bass
from concourse import mybir

F32 = mybir.dt.float32
F32R = mybir.dt.float32r
I32 = mybir.dt.int32
ALU = mybir.AluOpType
ACT = mybir.ActivationFunctionType
AX = mybir.AxisListType

P = 128
B, S, D = 8, 256, 256
N = B * S
TT = N // P
QT = S // P
KC = D // P
H, HD = 16, 16
HG = 4
CH = H // HG
GROUPS = H // HG
RING = 4
BY_POOL = (3, 4, 5)
EPS = 1e-5
BF16 = mybir.dt.bfloat16
F16 = mybir.dt.float16
E, F = 8, 1024
FC = F // P
SB = 256
L0_BLOCKS = (2 * N + E * (SB - 1)) // SB
SLOTS = L0_BLOCKS * SB
CT = 4
HALVES = L0_BLOCKS * SB // P


def spread(ap, axis, n):
    shape = list(ap.shape)
    return ap.unsqueeze(axis).broadcast_to(shape[:axis] + [n] + shape[axis:])


def wait(eng, sem, value):
    if isinstance(value, int) and value <= 0:
        return
    eng.wait_ge(sem, value)


def wait_apart(eng, sem, value, passed):
    eng.wait_ge(sem, value)
    eng.sem_inc(passed, 1)


def semaphores(nc, ctx):
    taken = []

    def clear():
        nc.clear_and_free_semaphores(taken)
        nc.all_engine_barrier()

    def sem(name):
        taken.append(nc.alloc_semaphore(name))
        return taken[-1]

    ctx.callback(clear)
    return sem


def split_matmul(pe, out, lhs, rhs, start, stop):
    pe.matmul(out, lhs[0], rhs[0], start=start, stop=False)
    pe.matmul(out, lhs[1], rhs[0], start=False, stop=False)
    return pe.matmul(out, lhs[0], rhs[1], start=False, stop=stop)


def attention_phase(nc, layer, shared, dram, load_x):
    x, ident, tanh_g = shared["x"], shared["ident"], shared["tanh_g"]
    tg = tanh_g[:, layer:layer + 1]

    with ExitStack() as ctx:
        def sb(name, shape, dt=F32):
            return ctx.enter_context(nc.sbuf_tensor(f"{name}_a{layer}", shape, dt))

        def ps(name, shape):
            return ctx.enter_context(nc.psum_tensor(f"{name}_a{layer}", shape, F32))

        new_sem = semaphores(nc, ctx)

        def sem(name):
            return new_sem(f"{name}_a{layer}")

        wq_raw, wk_raw = sb("wq_raw", [P, KC, D]), sb("wk_raw", [P, KC, D])
        wv_raw, wo_raw = sb("wv_raw", [P, KC, D]), sb("wo_raw", [P, KC, D])
        wq = [sb(f"wq{i}", [P, KC, CH * P], F32R) for i in range(2)]
        wk = [sb(f"wk{i}", [P, KC, CH * P], F32R) for i in range(2)]
        wv = [sb(f"wv{i}", [P, KC, D], F32R) for i in range(2)]
        wo = [sb(f"wo{i}", [P, KC, D], F32R) for i in range(2)]
        bq, bk = sb("bq", [P, CH]), sb("bk", [P, CH])
        bv, bo = sb("bv", [P, D]), sb("bo", [P, D])
        tgbo = sb("tgbo", [P, D])
        minus_half, eps_col = sb("minus_half", [P, QT]), sb("eps_col", [P, 1])
        lane = sb("lane", [P, H], I32)
        lane_low = sb("lane_low", [P, H], I32)
        is_head = sb("is_head", [P, H])
        low_bit = sb("low_bit", [P, 1], I32)
        minus_low = sb("minus_low", [P, 1])
        head_row = sb("head_row", [P, H, P], F32R)

        ctx_raw = [sb(f"ctx_raw{i}", [P, KC, S]) for i in range(2)]
        ctx_t = [sb(f"ctx_t{i}", [P, KC, S], F32R) for i in range(2)]
        stats, mean_var = sb("stats", [P, QT, 6]), sb("mean_var", [P, QT, 2])
        var_eps, rstd = sb("var_eps", [P, QT]), sb("rstd", [P, QT])
        xn = sb("xn", [P, QT, D])
        xn_t = [sb(f"xn_t{i}", [P, KC, S], F32R) for i in range(2)]
        q_full, k_full = sb("q_full", [P, CH, S]), sb("k_full", [P, CH, S])
        q_high = sb("q_high", [P, CH, S], F32R)
        q_st = [sb(f"q_st{i}", [P, CH, S], F32R) for i in range(2)]
        k_hi = [sb(f"k_hi{i}", [P, CH, S], F32R) for i in range(2)]
        k_lo = [sb(f"k_lo{i}", [P, CH, S], F32R) for i in range(2)]
        v_full = sb("v_full", [P, QT, H, HD])
        v = [sb(f"v{i}", [P, QT, H, P], F32R) for i in range(2)]
        mx = sb("mx", [P, H, QT])
        m_rep = sb("m_rep", [P, QT, HG, 2, H])
        m_t = sb("m_t", [P, S], F32R)
        prob = [sb(f"prob{i}", [P, 2, QT, S]) for i in range(2)]
        prob_hi = [sb(f"prob_hi{i}", [P, 2, QT, S], F32R) for i in range(RING)]
        prob_lo = [sb(f"prob_lo{i}", [P, 2, QT, S], F32R) for i in range(RING)]
        head_t = [sb(f"head_t{i}", [P, S]) for i in range(2)]
        rsum, o = sb("rsum", [P, QT, HG]), sb("o", [P, QT, D])
        o_t = [sb(f"o_t{i}", [P, KC, S], F32R) for i in range(2)]

        if not load_x:
            rows = [sb(f"rows{i}", [P, 2, QT, D]) for i in range(2)]
            row_index = [sb(f"row_index{i}", [P, 2, QT], I32) for i in range(2)]
            rows_ld = [sem("rows_ld0"), sem("rows_ld1")]
            rows_indexed, half_combined, combined = sem("rows_indexed"), sem("half_combined"), sem("combined")

        ps_st = [ps(f"ps_st{i}", [P, 2, QT, S]) for i in range(2)]
        bank_a, bank_b = ps("bank_a", [P, 512]), ps("bank_b", [P, 512])
        ps_head = ps("ps_head", [P, 512])
        ps_o = ps("ps_o", [P, 4, HG, 32])

        w_ld, q_ld, rest_ld = sem("w_ld"), sem("q_ld"), sem("rest_ld")
        x_ld = [sem("x_ld0"), sem("x_ld1")]
        ctx_ld = [sem("ctx_ld0"), sem("ctx_ld1")]
        pool_const, dve_const, wq_ready, wk_ready, wv_ready, wo_ready, tgbo_ready = (
            sem(n) for n in ("pool_const", "dve_const", "wq_ready", "wk_ready", "wv_ready", "wo_ready", "tgbo_ready"))
        dve_passed, pool_passed = sem("dve_passed"), sem("pool_passed")
        wq_hi, wk_hi, wv_hi, wo_hi = sem("wq_hi"), sem("wk_hi"), sem("wv_hi"), sem("wo_hi")
        ln_stats, ln_mean, ln_eps, ln_rstd, xn_ready = (
            sem(n) for n in ("ln_stats", "ln_mean", "ln_eps", "ln_rstd", "xn_ready"))
        bias_added, ctx_hi, ctx_ready = sem("bias_added"), sem("ctx_hi"), sem("ctx_ready")
        xt_ps, xt_hi, xt_ready = sem("xt_ps"), sem("xt_hi"), sem("xt_ready")
        q_ps, q_biased, q_rounded, q_ready = sem("q_ps"), sem("q_biased"), sem("q_rounded"), sem("q_ready")
        k_ps, k_biased, k_rounded, k_ready = sem("k_ps"), sem("k_biased"), sem("k_rounded"), sem("k_ready")
        v_ps, v_ready = sem("v_ps"), sem("v_ready")
        s_ps, max_done, m_hi, m_ready, mt_ps, mt_ready = (
            sem(n) for n in ("s_ps", "max_done", "m_hi", "m_ready", "mt_ps", "mt_ready"))
        prob_full, lo_dve, lo_pool, v_full_ready, v_rounded = (
            sem(n) for n in ("prob_full", "lo_dve", "lo_pool", "v_full_ready", "v_rounded"))
        st_ps, prob_ready, pv_done, head_out, turned, sum_inv, o_ready = (
            sem(n) for n in ("st_ps", "prob_ready", "pv_done", "head_out", "turned", "sum_inv", "o_ready"))
        ot_ps, ot_hi, ot_ready, out_ps, x_done = (
            sem(n) for n in ("ot_ps", "ot_hi", "ot_ready", "out_ps", "x_done"))

        def x_tiles(b):
            return x[:, bass.ds(b * QT, QT), :] if not isinstance(b, int) else x[:, b * QT:b * QT + QT, :]

        PER_POOL = len(BY_POOL)
        PER_DVE = H // 2 - PER_POOL

        def split_wait(eng, b, j):
            if j < 0:
                b, j = b - 1, j + H // 2
            if j in BY_POOL:
                wait(eng, lo_pool, b * PER_POOL + BY_POOL.index(j) + 1)
            else:
                wait(eng, lo_dve, b * PER_DVE + sum(i not in BY_POOL for i in range(j)) + 1)

        def split_prob(eng, b, j):
            eng.wait_ge(prob_ready, b * 8 + j + 1)
            wait(eng, pv_done, b * 8 + j - RING + 1)
            eng.tensor_tensor(prob_lo[j % RING][:, :, :, :], prob[j % 2][:, :, :, :],
                              prob_hi[j % RING][:, :, :, :].bitcast(F32),
                              ALU.subtract).then_inc(lo_pool if j in BY_POOL else lo_dve, 1)

        block = ctx.enter_context(nc.Block())

        @block.sync
        def _(sp):
            if load_x:
                src = dram["x"].rearrange("(t p) d -> p t d", p=P)
                sp.dma_start(x[:, 0:QT, :], src[:, 0:QT, :]).then_inc(x_ld[0], 16)
            w3 = [dram[n].rearrange("(k p) n -> p k n", p=P) for n in ("wq", "wk", "wv", "wo")]
            sp.dma_start(wq_raw[:, :, :], w3[0]).then_inc(q_ld, 16)
            sp.dma_start(bq[:, :], dram["bq"]).then_inc(q_ld, 16)
            sp.dma_start(bk[:, :], dram["bk"]).then_inc(w_ld, 16)
            sp.dma_start(wk_raw[:, :, :], w3[1]).then_inc(w_ld, 16)
            ctx_src = dram["ctx_t"].rearrange("(k p) n -> p k n", p=P)
            sp.dma_start(ctx_raw[0][:, :, :], ctx_src[:, :, 0:S]).then_inc(ctx_ld[0], 16)
            sp.dma_start(wv_raw[:, :, :], w3[2]).then_inc(rest_ld, 16)
            sp.dma_start(wo_raw[:, :, :], w3[3]).then_inc(rest_ld, 16)
            sp.dma_start(bv[:, :], dram["bv"]).then_inc(rest_ld, 16)
            sp.dma_start(bo[:, :], dram["bo"]).then_inc(rest_ld, 16)
            if load_x:
                sp.dma_start(x[:, QT:TT, :], src[:, QT:TT, :]).then_inc(x_ld[1], 16)
            sp.dma_start(ctx_raw[1][:, :, :], ctx_src[:, :, S:2 * S]).then_inc(ctx_ld[1], 16)
            with sp.Fori(1, B // 2) as t:
                for i in range(2):
                    sp.wait_ge(ctx_ready, t * 2 - 1 + i)
                    sp.dma_start(ctx_raw[i][:, :, :], ctx_src[:, :, bass.ds(t * (2 * S) + i * S, S)]).then_inc(ctx_ld[i], 16)

        @block.gpsimd
        def _(pool):
            pool.memset(minus_half[:, :], -0.5).then_inc(pool_const, 1)
            pool.iota(lane[:, :], pattern=[[-1, H]], base=H, channel_multiplier=1).then_inc(pool_const, 1)

            def inverse_deviation(b):
                wait_apart(pool, ln_mean, b * QT + QT, pool_passed)
                pool.tensor_scalar(var_eps[:, :], mean_var[:, :, 1], EPS, None, ALU.add).then_inc(ln_eps, 1)
                pool.wait_ge(ln_eps, b + 1)
                pool.tensor_tensor(rstd[:, :], var_eps[:, :], minus_half[:, :], ALU.pow).then_inc(ln_rstd, 1)

            def add_bias(b):
                pool.wait_ge(xn_ready, b * QT + QT)
                pool.wait_ge(tgbo_ready, 1)
                pool.tensor_tensor(x_tiles(b), x_tiles(b), spread(tgbo[:, :], 1, QT), ALU.add).then_inc(bias_added, 1)

            def context_high(b, par, half):
                wait(pool, k_ps, b * 2)
                wait_apart(pool, ctx_ld[par], (half + 1) * 16, pool_passed)
                pool.tensor_copy(ctx_t[0][:, :, :], ctx_raw[par][:, :, :]).then_inc(ctx_hi, 1)

            def context_low(b, par):
                pool.wait_ge(ctx_hi, b + 1)
                pool.tensor_tensor(ctx_t[1][:, :, :], ctx_raw[par][:, :, :], ctx_t[0][:, :, :].bitcast(F32),
                                   ALU.subtract).then_inc(ctx_ready, 1)

            def of_group(part, g):
                return part[:, :, :, :].rearrange("p k (c g) n -> p k c g n", g=HG)[:, :, :, g, :]

            def keys_low(b, par):
                wait(pool, pv_done, (b - 1) * 8)
                for u in range(2):
                    cs = slice(2 * u, 2 * u + 2)
                    pool.wait_ge(k_rounded, b * 2 + u + 1)
                    pool.tensor_tensor(k_lo[par][:, cs, :], k_full[:, cs, :], k_hi[par][:, cs, :].bitcast(F32),
                                       ALU.subtract).then_inc(k_ready, 1)

            def values(b):
                wait(pool, pv_done, b * 8)
                wait_apart(pool, v_full_ready, b + 1, pool_passed)
                for g in range(HG):
                    full = v_full[:, :, :, :].rearrange("p k (c g) d -> p k c g d", g=HG)[:, :, :, g, :]
                    high, low = (of_group(v[i], g)[:, :, :, 32 * g:32 * g + HD] for i in range(2))
                    pool.tensor_copy(high, full).then_inc(v_rounded, 1)
                    pool.wait_ge(v_rounded, b * HG + g + 1)
                    ins = pool.tensor_tensor(low, full, high.bitcast(F32), ALU.subtract)
                ins.then_inc(v_ready, 1)

            def gather_rows(b, par):
                if load_x:
                    return
                if not (isinstance(b, int) and b < 2):
                    wait_apart(pool, combined, b - 1, pool_passed)
                for i in range(2):
                    pool.tensor_copy(row_index[par][:, i, :], shared["slot"][i][:, bass.ds(b * QT, QT)]).then_inc(rows_indexed, 1)
                wait_apart(pool, rows_indexed, b * 2 + 2, pool_passed)
                for i in range(2):
                    for q in range(QT):
                        pool.indirect_dma_start(
                            out=rows[par][:, i, q, :], out_offset=None, in_=dram["ye"],
                            in_offset=bass.IndirectOffsetOnAxis(ap=row_index[par][:, i, q:q + 1], axis=0)).then_inc(rows_ld[par], 16)

            def body(b, par, half, more=True, last=False):
                if not last:
                    keys_low(b - 1, 1 - par)
                if more:
                    inverse_deviation(b)
                split_prob(pool, b - 2, BY_POOL[0])
                split_prob(pool, b - 2, BY_POOL[1])
                if more:
                    add_bias(b)
                split_prob(pool, b - 2, BY_POOL[2])
                if more:
                    context_high(b, par, half)
                    context_low(b, par)
                    if not (isinstance(b, int) and b + 1 >= B):
                        gather_rows(b + 1, 1 - par)
                if not last:
                    values(b - 1)

            if not load_x:
                pool.wait_ge(shared["cleared"], 16)
            gather_rows(0, 0)
            inverse_deviation(0)
            gather_rows(1, 1)
            context_high(0, 0, 0)
            context_low(0, 0)
            add_bias(0)
            for i in range(2):
                pool.memset(v[i][:, :, :, :].bitcast(F32), 0.0).then_inc(pool_const, 1)
            pool.wait_ge(pool_const, 4)
            for g in range(HG):
                pool.memset(of_group(v[0], g)[:, :, :, 32 * g + HD:32 * g + HD + 1].bitcast(F32), 1.0).then_inc(pool_const, 1)
            inverse_deviation(1)
            keys_low(0, 0)
            values(0)
            add_bias(1)
            context_high(1, 1, 0)
            context_low(1, 1)
            gather_rows(2, 0)
            body(2, 0, 1)
            with pool.Fori(1, B // 2 - 1) as t:
                body(t * 2 + 1, 1, t)
                body(t * 2 + 2, 0, t + 1)
            body(B - 1, 1, B // 2 - 1)
            body(B, 0, None, more=False)
            body(B + 1, 1, None, more=False, last=True)

        @block.scalar
        def _(act):
            def project(b, u, ps_sem, done_sem, consumed, bias, full):
                bank = bank_a if u else bank_b
                act.wait_ge(ps_sem, b * 2 + u + 1)
                wait(act, consumed, b * 2 + u - 1)
                for c in range(2):
                    ins = act.activation(full[:, 2 * u + c, :], bank[:, c * S:(c + 1) * S], ACT.Identity,
                                         bias=bias[:, 2 * u + c:2 * u + c + 1])
                ins.then_inc(done_sem, 1)

            def queries(b, u):
                project(b, u, q_ps, q_biased, q_ready, bq, q_full)

            def keys(b, u):
                project(b, u, k_ps, k_biased, k_ready, bk, k_full)

            def inputs(b):
                act.wait_ge(xt_ps, b + 1)
                act.activation(xn_t[0][:, :, :], bank_a[:, :].rearrange("p (k s) -> p k s", k=KC),
                               ACT.Copy).then_inc(xt_hi, 1)

            def maxima(b):
                act.wait_ge(mt_ps, b + 1)
                act.activation(m_t[:, :], bank_b[:, 0:S], ACT.Copy).then_inc(mt_ready, 1)

            def out_hi(b):
                act.wait_ge(ot_ps, b + 1)
                act.activation(o_t[0][:, :, :], bank_a[:, :].rearrange("p (k s) -> p k s", k=KC),
                               ACT.Copy).then_inc(ot_hi, 1)

            def probabilities(b, j):
                act.wait_ge(st_ps, b * 8 + j + 1)
                split_wait(act, b, j - 2)
                act.activation(prob[j % 2][:, :, :, :], ps_st[j % 2][:, :, :, :], ACT.Exp,
                               scale=HD ** -0.5).then_inc(prob_full, 1)
                wait(act, pv_done, b * 8 + j - RING + 1)
                act.activation(prob_hi[j % RING][:, :, :, :], ps_st[j % 2][:, :, :, :], ACT.Exp,
                               scale=HD ** -0.5).then_inc(prob_ready, 1)

            def head_copy(b, g):
                act.wait_ge(pv_done, b * 8 + 2 * g + 2)
                wait(act, turned, b * GROUPS + g - 1)
                act.activation(head_t[g % 2][:, :], ps_head[:, 0:S], ACT.Copy).then_inc(head_out, 1)

            def body(b, first=False, last=False, more=True):
                if not last:
                    queries(b + 1, 0)
                probabilities(b, 0)
                if not last:
                    queries(b + 1, 1)
                    keys(b + 1, 0)
                probabilities(b, 1)
                if not last:
                    keys(b + 1, 1)
                if not first:
                    out_hi(b - 1)
                probabilities(b, 2)
                head_copy(b, 0)
                for j in range(3, 6):
                    probabilities(b, j)
                head_copy(b, 1)
                probabilities(b, 6)
                probabilities(b, 7)
                head_copy(b, 2)
                if not last:
                    if more:
                        inputs(b + 2)
                    maxima(b + 1)
                head_copy(b, 3)

            act.wait_ge(q_ld, 32)
            act.wait_ge(w_ld, 32)
            inputs(0)
            queries(0, 0)
            queries(0, 1)
            keys(0, 0)
            keys(0, 1)
            inputs(1)
            maxima(0)
            body(0, first=True)
            with act.Fori(1, B - 2) as b:
                body(b)
            body(B - 2, more=False)
            body(B - 1, last=True)
            out_hi(B - 1)

        @block.vector
        def _(dve):
            def spread_weight(raw, parts, hi_sem, ready_sem):
                for k in range(KC):
                    src = raw[:, k, :].rearrange("p (h d) -> p h d", d=HD)
                    for r in range(2):
                        ins = dve.tensor_copy(parts[0][:, k, :].rearrange("p (h r d) -> p h r d", r=2, d=HD)[:, :, r, :], src)
                ins.then_inc(hi_sem, 1)
                dve.wait_ge(hi_sem, 1)
                for k in range(KC):
                    src = raw[:, k, :].rearrange("p (h d) -> p h d", d=HD)
                    for r in range(2):
                        hi, lo = (w[:, k, :].rearrange("p (h r d) -> p h r d", r=2, d=HD)[:, :, r, :] for w in parts)
                        ins = dve.tensor_tensor(lo, src, hi.bitcast(F32), ALU.subtract)
                ins.then_inc(ready_sem, 1)

            def weight(raw, parts, hi_sem, ready_sem):
                dve.tensor_copy(parts[0][:, :, :], raw[:, :, :]).then_inc(hi_sem, 1)
                dve.wait_ge(hi_sem, 1)
                dve.tensor_tensor(parts[1][:, :, :], raw[:, :, :], parts[0][:, :, :].bitcast(F32),
                                  ALU.subtract).then_inc(ready_sem, 1)

            def combine(b, par, half):
                if load_x:
                    return
                dve.wait_ge(rows_ld[par], half * (32 * QT) + 32 * QT)
                for i in range(2):
                    if i:
                        dve.wait_ge(half_combined, b + 1)
                    for q in range(QT):
                        tile = x[:, bass.ds(b * QT + q, 1), :].rearrange("p t d -> p (t d)")
                        ins = dve.scalar_tensor_tensor(tile, rows[par][:, i, q, :], shared["weight"][i][:, bass.ds(b * QT + q, 1)],
                                                       tile, ALU.mult, ALU.add)
                    ins.then_inc(combined if i else half_combined, 1)
                if isinstance(b, int):
                    dve.wait_ge(combined, b + 1)
                else:
                    wait_apart(dve, combined, b + 1, dve_passed)

            def moments(b):
                for q in range(QT):
                    dve.bn_stats(stats[:, q, :], x_tile(b, q)).then_inc(ln_stats, 1)
                wait_apart(dve, ln_stats, b * QT + QT, dve_passed)
                for q in range(QT):
                    dve.bn_aggr(mean_var[:, q, :], stats[:, q, :]).then_inc(ln_mean, 1)

            def normalise_rows(b):
                dve.wait_ge(ln_rstd, b + 1)
                wait(dve, xt_ps, b)
                for q in range(QT):
                    dve.tensor_scalar(xn[:, q:q + 1, :], x_tile(b, q), mean_var[:, q, 0:1], rstd[:, q:q + 1],
                                      ALU.subtract, ALU.mult).then_inc(xn_ready, 1)

            def x_tile(b, q):
                return x[:, bass.ds(b * QT + q, 1), :] if not isinstance(b, int) else x[:, b * QT + q:b * QT + q + 1, :]

            def low_part(full, parts, hi_sem, done_sem, count):
                dve.wait_ge(hi_sem, count)
                dve.tensor_tensor(parts[1][:, :, :], full[:, :].rearrange("p (k s) -> p k s", k=KC),
                                  parts[0][:, :, :].bitcast(F32), ALU.subtract).then_inc(done_sem, 1)

            def queries(b, par, u):
                cs = slice(2 * u, 2 * u + 2)
                dve.wait_ge(q_biased, b * 2 + u + 1)
                dve.tensor_copy(q_high[:, cs, :], q_full[:, cs, :]).then_inc(q_rounded, 1)
                dve.wait_ge(q_rounded, b * 2 + u + 1)
                dve.scalar_tensor_tensor(q_st[par][:, cs, :], q_high[:, cs, :].bitcast(F32), minus_low[:, 0:1],
                                         q_full[:, cs, :], ALU.mult, ALU.add).then_inc(q_ready, 1)

            def keys(b, par, u):
                cs = slice(2 * u, 2 * u + 2)
                dve.wait_ge(k_biased, b * 2 + u + 1)
                dve.tensor_copy(k_hi[par][:, cs, :], k_full[:, cs, :]).then_inc(k_rounded, 1)

            def values(b):
                dve.wait_ge(v_ps, b + 1)
                wait(dve, v_ready, b)
                for kt in range(QT):
                    ins = dve.tensor_tensor(v_full[:, kt, :, :],
                                            ps_head[:, kt * D:(kt + 1) * D].rearrange("p (h d) -> p h d", d=HD),
                                            bv[:, :].rearrange("p (h d) -> p h d", d=HD), ALU.add)
                ins.then_inc(v_full_ready, 1)

            def take_maxima(b, i):
                for h in (2 * i, 2 * i + 1):
                    dve.wait_ge(s_ps, b * H + h + 1)
                    bank = bank_a if h % 2 else bank_b
                    dve.tensor_reduce(mx[:, h, :], bank[:, :].rearrange("p (q s) -> p q s", q=QT), AX.X,
                                      ALU.max).then_inc(max_done, 1)

            def negate(b):
                dve.wait_ge(max_done, b * H + H)
                src = spread(mx[:, :, :].rearrange("p h q -> p q h"), 2, HG)
                dve.tensor_scalar(m_rep[:, :, :, 0, :].bitcast(F32R), src, -1.0, None, ALU.mult).then_inc(m_hi, 1)
                dve.wait_ge(m_hi, b + 1)
                for q in range(QT):
                    ins = dve.scalar_tensor_tensor(m_rep[:, q, :, 1, :], src[:, q, :, :], -1.0, m_rep[:, q, :, 0, :],
                                                   ALU.mult, ALU.subtract)
                ins.then_inc(m_ready, 1)

            def normalise(b, g):
                dve.wait_ge(turned, b * GROUPS + g + 1)
                tiles = slice(g % 2 * QT, g % 2 * QT + QT)
                dve.reciprocal(rsum[:, :, :], ps_o[:, tiles, :, HD]).then_inc(sum_inv, 1)
                dve.wait_ge(sum_inv, b * GROUPS + g + 1)
                if g == 0:
                    wait(dve, ot_ps, b)
                for q in range(QT):
                    ins = dve.tensor_tensor(o[:, q, g * HG * HD:(g + 1) * HG * HD].rearrange("p (h d) -> p h d", d=HD),
                                            ps_o[:, g % 2 * QT + q, :, 0:HD], spread(rsum[:, q, :], 2, HD), ALU.mult)
                ins.then_inc(o_ready, 1)

            def residual(b):
                dve.wait_ge(out_ps, b + 1)
                dve.wait_ge(bias_added, b + 1)
                dve.scalar_tensor_tensor(x_tiles(b), bank_b[:, :].rearrange("p (q d) -> p q d", q=QT), tg, x_tiles(b),
                                         ALU.mult, ALU.add).then_inc(x_done, 1)

            def body(b, par, half, first=False, last=False, more=True):
                if not last:
                    queries(b + 1, 1 - par, 0)
                if not first:
                    normalise(b - 1, GROUPS - 1)
                split_prob(dve, b, 0)
                if not last:
                    queries(b + 1, 1 - par, 1)
                    values(b + 1)
                    keys(b + 1, 1 - par, 0)
                if more:
                    combine(b + 2, par, half + 1)
                split_prob(dve, b, 1)
                if not last:
                    keys(b + 1, 1 - par, 1)
                if not first:
                    low_part(bank_a, o_t, ot_hi, ot_ready, b)
                if more:
                    moments(b + 2)
                split_prob(dve, b, 2)
                if not first:
                    residual(b - 1)
                normalise(b, 0)
                if not last:
                    take_maxima(b + 1, 0)
                    take_maxima(b + 1, 1)
                if more:
                    normalise_rows(b + 2)
                if not last:
                    for i in range(2, 5):
                        take_maxima(b + 1, i)
                normalise(b, 1)
                if not last:
                    take_maxima(b + 1, 5)
                    take_maxima(b + 1, 6)
                split_prob(dve, b, 6)
                if not last:
                    take_maxima(b + 1, 7)
                    negate(b + 1)
                split_prob(dve, b, 7)
                if more:
                    low_part(bank_a, xn_t, xt_hi, xt_ready, b + 3)
                normalise(b, 2)

            if load_x:
                dve.wait_ge(x_ld[0], 16)
            combine(0, 0, 0)
            moments(0)
            normalise_rows(0)
            dve.wait_ge(q_ld, 32)
            spread_weight(wq_raw, wq, wq_hi, wq_ready)
            low_part(bank_a, xn_t, xt_hi, xt_ready, 1)
            dve.wait_ge(w_ld, 32)
            spread_weight(wk_raw, wk, wk_hi, wk_ready)
            dve.wait_ge(pool_const, 2)
            dve.tensor_scalar(lane_low[:, :], lane[:, :], 15, None, ALU.bitwise_and).then_inc(dve_const, 1)
            dve.tensor_scalar(low_bit[:, :], lane[:, 0:1], 16, None, ALU.bitwise_and).then_inc(dve_const, 1)
            dve.wait_ge(dve_const, 2)
            dve.tensor_scalar(is_head[:, :], lane_low[:, :], 0.0, None, ALU.is_equal).then_inc(dve_const, 1)
            dve.tensor_scalar(minus_low[:, :], low_bit[:, :], 1.0 / 16, -1.0, ALU.mult, ALU.add).then_inc(dve_const, 1)
            dve.wait_ge(dve_const, 4)
            dve.tensor_copy(head_row[:, :, :], spread(is_head[:, :], 2, P)).then_inc(dve_const, 1)
            dve.wait_ge(rest_ld, 64)
            weight(wv_raw, wv, wv_hi, wv_ready)
            weight(wo_raw, wo, wo_hi, wo_ready)
            dve.tensor_scalar(tgbo[:, :], bo[:, :], tg, None, ALU.mult).then_inc(tgbo_ready, 1)
            if load_x:
                dve.wait_ge(x_ld[1], 16)
            combine(1, 1, 0)
            moments(1)
            queries(0, 0, 0)
            queries(0, 0, 1)
            values(0)
            keys(0, 0, 0)
            keys(0, 0, 1)
            for i in range(H // 2):
                take_maxima(0, i)
                if i == 4:
                    normalise_rows(1)
            negate(0)
            low_part(bank_a, xn_t, xt_hi, xt_ready, 2)
            body(0, 0, 0, first=True)
            with dve.Fori(0, B // 2 - 2) as t:
                body(t * 2 + 1, 1, t)
                body(t * 2 + 2, 0, t + 1)
            body(B - 3, 1, (B - 3) // 2)
            body(B - 2, 0, (B - 2) // 2, more=False)
            body(B - 1, 1, (B - 1) // 2, last=True, more=False)
            normalise(B - 1, GROUPS - 1)
            low_part(bank_a, o_t, ot_hi, ot_ready, B)
            residual(B - 1)

        @block.tensor
        def _(pe):
            def turn(src, bank):
                for q in range(QT):
                    for k in range(KC):
                        ins = pe.transpose(bank[:, k * S + q * P:k * S + (q + 1) * P], src[:, q, k * P:(k + 1) * P], ident[:, :])
                return ins

            def x_transpose(b):
                pe.wait_ge(xn_ready, b * QT + QT)
                wait(pe, max_done, b * H)
                turn(xn, bank_a).then_inc(xt_ps, 1)

            def max_transpose(b):
                pe.wait_ge(m_ready, b + 1)
                for q in range(QT):
                    ins = pe.transpose(bank_b[:, q * P:(q + 1) * P],
                                       m_rep[:, q, :, :, :].rearrange("p g r h -> p (g r h)"), ident[:, :])
                ins.then_inc(mt_ps, 1)

            def o_transpose(b, x_next):
                pe.wait_ge(o_ready, (b + 1) * GROUPS)
                if x_next is None:
                    wait(pe, ot_ready, b)
                else:
                    pe.wait_ge(k_biased, x_next * 2 + 2)
                turn(o, bank_a).then_inc(ot_ps, 1)

            def heads_project(w, src, bank, u, done):
                for c in range(2):
                    for k in range(KC):
                        cols = slice((2 * u + c) * P, (2 * u + c + 1) * P)
                        ins = split_matmul(pe, bank[:, c * S:(c + 1) * S], [w[i][:, k, cols] for i in range(2)],
                                           [src[i][:, k, :] for i in range(2)], k == 0, k == KC - 1)
                ins.then_inc(done, 1)

            def queries(b, u):
                if u == 0:
                    pe.wait_ge(xt_ready, b + 1)
                    wait(pe, mt_ready, b)
                heads_project(wq, xn_t, bank_a if u else bank_b, u, q_ps)

            def keys(b, u):
                pe.wait_ge(ctx_ready, b + 1)
                pe.wait_ge(q_biased, b * 2 + u + 1)
                heads_project(wk, ctx_t, bank_a if u else bank_b, u, k_ps)

            def token_major(parts, w, bank, done):
                for q in range(QT):
                    for k in range(KC):
                        ins = split_matmul(pe, bank[:, q * D:(q + 1) * D],
                                           [parts[i][:, k, q * P:(q + 1) * P] for i in range(2)],
                                           [w[i][:, k, :] for i in range(2)], k == 0, k == KC - 1)
                ins.then_inc(done, 1)

            def out_project(b, k_next):
                pe.wait_ge(ot_ready, b + 1)
                if k_next is None:
                    wait(pe, x_done, b)
                else:
                    pe.wait_ge(k_biased, k_next * 2 + 1)
                token_major(o_t, wo, bank_b, out_ps)

            def value_project(b):
                pe.wait_ge(ctx_ready, b + 1)
                wait(pe, head_out, (b - 1) * GROUPS)
                token_major(ctx_t, wv, ps_head, v_ps)

            def head_scores(b, par, i):
                for h in (2 * i, 2 * i + 1):
                    bank = bank_a if h % 2 else bank_b
                    if h == 0:
                        pe.wait_ge(q_ready, b * 2 + 2)
                        pe.wait_ge(k_rounded, b * 2 + 2)
                        wait(pe, x_done, b - 1)
                    elif h == 1:
                        wait(pe, ot_ready, b - 1)
                    else:
                        pe.wait_ge(max_done, b * H + h - 1)
                    c, g = h // HG, h % HG
                    rows = slice(32 * g, 32 * g + 32)
                    for q in range(QT):
                        ins = pe.matmul(bank[:, q * S:(q + 1) * S], q_st[par][rows, c, q * P:(q + 1) * P],
                                        k_hi[par][rows, c, :], start=True, stop=True)
                    ins.then_inc(s_ps, 1)

            def pair_scores(b, par, j):
                wait(pe, prob_ready, b * 8 + j - 1)
                heads = [(e, (2 * j + e) // HG, (2 * j + e) % HG) for e in range(2)]
                for e, c, g in heads:
                    rows = slice(32 * g, 32 * g + 32)
                    pe.matmul(ps_st[j % 2][:, e, :, :], head_row[rows, 2 * j + e, :], spread(m_t[rows, :], 1, QT),
                              start=True, stop=False)
                for kt in range(QT):
                    for k_part in (k_hi, k_lo):
                        for e, c, g in heads:
                            rows = slice(32 * g, 32 * g + 32)
                            ins = pe.matmul(ps_st[j % 2][:, e, kt, :], k_part[par][rows, c, kt * P:(kt + 1) * P],
                                            q_st[par][rows, c, :], start=False, stop=kt == QT - 1 and k_part is k_lo)
                ins.then_inc(st_ps, 1)

            def weigh_values(b, par, j, v_out=0):
                split_wait(pe, b, j)
                if j == 0:
                    pe.wait_ge(v_ready, b + 1)
                    wait(pe, v_full_ready, v_out)
                if j % 2 == 0:
                    wait(pe, head_out, b * GROUPS + j // 2)
                for h in (2 * j, 2 * j + 1):
                    for kt in range(QT):
                        for p_part, v_part in ((prob_hi, 0), (prob_lo, 0), (prob_hi, 1)):
                            ins = pe.matmul(ps_head[:, 0:S], v[v_part][:, kt, h, :], p_part[j % RING][:, h % 2, kt, :],
                                            start=h % HG == 0 and kt == 0 and p_part is prob_hi and v_part == 0,
                                            stop=h % HG == HG - 1 and kt == QT - 1 and v_part == 1)
                ins.then_inc(pv_done, 1)

            def turn_heads(b, g):
                wait(pe, o_ready, b * GROUPS + g)
                pe.wait_ge(head_out, b * GROUPS + g + 1)
                for q in range(QT):
                    ins = pe.transpose(ps_o[:, g % 2 * QT + q, :, :].rearrange("p h w -> p (h w)"),
                                       head_t[g % 2][:, q * P:(q + 1) * P], ident[:, :])
                ins.then_inc(turned, 1)

            def body(b, par, first=False, last=False, more=True):
                def maxima(i):
                    if not last:
                        head_scores(b + 1, 1 - par, i)

                if first:
                    pe.wait_ge(dve_const, 5)
                if not last:
                    queries(b + 1, 0)
                if not first:
                    turn_heads(b - 1, 3)
                pe.wait_ge(k_ready, b * 2 + 2)
                pe.wait_ge(mt_ready, b + 1)
                pair_scores(b, par, 0)
                if not last:
                    queries(b + 1, 1)
                    value_project(b + 1)
                    keys(b + 1, 0)
                pair_scores(b, par, 1)
                if not last:
                    keys(b + 1, 1)
                weigh_values(b, par, 0, 0 if last else b + 2)
                if not first:
                    o_transpose(b - 1, None if last else b + 1)
                pair_scores(b, par, 2)
                weigh_values(b, par, 1)
                if not first:
                    out_project(b - 1, None if last else b + 1)
                turn_heads(b, 0)
                pair_scores(b, par, 3)
                maxima(0)
                weigh_values(b, par, 2)
                maxima(1)
                pair_scores(b, par, 4)
                maxima(2)
                pair_scores(b, par, 5)
                maxima(3)
                weigh_values(b, par, 3)
                maxima(4)
                pair_scores(b, par, 6)
                turn_heads(b, 1)
                maxima(5)
                weigh_values(b, par, 4)
                maxima(6)
                pair_scores(b, par, 7)
                maxima(7)
                weigh_values(b, par, 5)
                if more:
                    x_transpose(b + 2)
                turn_heads(b, 2)
                weigh_values(b, par, 6)
                if not last:
                    max_transpose(b + 1)
                weigh_values(b, par, 7)

            x_transpose(0)
            pe.wait_ge(wq_ready, 1)
            queries(0, 0)
            queries(0, 1)
            pe.wait_ge(wv_ready, 1)
            value_project(0)
            pe.wait_ge(wk_ready, 1)
            keys(0, 0)
            keys(0, 1)
            for i in range(H // 2):
                head_scores(0, 0, i)
            x_transpose(1)
            max_transpose(0)
            pe.wait_ge(wo_ready, 1)
            body(0, 0, first=True)
            with pe.Fori(0, B // 2 - 2) as t:
                body(t * 2 + 1, 1)
                body(t * 2 + 2, 0)
            body(B - 3, 1)
            body(B - 2, 0, more=False)
            body(B - 1, 1, last=True, more=False)
            turn_heads(B - 1, 3)
            o_transpose(B - 1, None)
            out_project(B - 1, None)


def constants_phase(nc, shared, dram):
    with ExitStack() as ctx:
        gates = ctx.enter_context(nc.sbuf_tensor("gates_sb", [P, 4], F32))
        sem = semaphores(nc, ctx)
        g_ld, zeroed, ident_ready, tanh_done = (
            sem(n) for n in ("g_ld", "zeroed", "ident_ready", "tanh_done"))
        block = ctx.enter_context(nc.Block())

        @block.sync
        def _(sp):
            sp.dma_start(gates[:, :], dram["gates"]).then_inc(g_ld, 16)
            sp.wait_ge(zeroed, 3)
            sp.dma_start(dram["ye"][SLOTS:SLOTS + 1, :], shared["zeros"][0:1, :]).then_inc(shared["cleared"], 16)

        @block.scalar
        def _(act):
            act.wait_ge(g_ld, 16)
            act.activation(shared["tanh_g"][:, :], gates[:, :], ACT.Tanh).then_inc(tanh_done, 1)
            act.wait_ge(tanh_done, 1)

        @block.gpsimd
        def _(pool):
            pool.memset(shared["ident"][:, :], 0.0).then_inc(zeroed, 1)
            pool.memset(shared["zeros"][:, :], 0.0).then_inc(zeroed, 1)
            pool.memset(shared["ones"][:, :], 1.0).then_inc(zeroed, 1)
            pool.wait_ge(zeroed, 3)
            pool.affine_select(out=shared["ident"][:, :], in_=shared["ident"][:, :], compare_op=ALU.not_equal, fill=1.0,
                               base=0, pattern=[[-1, P]], channel_multiplier=1).then_inc(ident_ready, 1)
            pool.affine_select(out=shared["before"][:, :], in_=shared["ones"][:, :], compare_op=ALU.is_gt, fill=0.0,
                               base=0, pattern=[[1, P]], channel_multiplier=-1).then_inc(ident_ready, 1)
            pool.iota(shared["expert_no"][:, :], pattern=[[1, E]], base=0, channel_multiplier=0).then_inc(ident_ready, 1)
            pool.iota(shared["block_no"][:, :], pattern=[[1, L0_BLOCKS]], base=0, channel_multiplier=0).then_inc(ident_ready, 1)
            pool.iota(shared["row_no"][:, :], pattern=[[1, 1]], base=0, channel_multiplier=1).then_inc(ident_ready, 1)
            pool.iota(shared["lane_no"][:, :], pattern=[[1, P]], base=0, channel_multiplier=0).then_inc(ident_ready, 1)
            pool.iota(shared["token_no"][:, :], pattern=[[P, TT]], base=0, channel_multiplier=1).then_inc(ident_ready, 1)
            pool.wait_ge(ident_ready, 7)


def expert_buffers(nc, ctx, layer):
    sem = semaphores(nc, ctx)

    def pair(name, shape, dt=F32):
        return [ctx.enter_context(nc.sbuf_tensor(f"{name}{i}_w{layer}", shape, dt)) for i in range(2)]

    return {"w1_raw": pair("w1_raw", [P, KC * F + (0 if layer else FC)]),
            "w2_raw": pair("w2_raw", [P, FC * D + (0 if layer else D)]),
            "w1_index": pair("w1_index", [P, 1], I32), "w2_index": pair("w2_index", [P, 1], I32),
            "w1_ld": [sem(f"w1_ld{i}_w{layer}") for i in range(2)], "w2_ld": [sem(f"w2_ld{i}_w{layer}") for i in range(2)],
            "w1_indexed": sem(f"w1_indexed_w{layer}"), "w2_indexed": sem(f"w2_indexed_w{layer}"),
            "passed": sem(f"passed_w{layer}")}


def gather_weights(pool, which, buffers, shared, dram, b, i):
    index, indexed = buffers[which + "_index"][i], buffers[which + "_indexed"]
    pool.tensor_copy(index[:, :], shared["block_row"][:, bass.ds(b, 1)]).then_inc(indexed, 1)
    wait_apart(pool, indexed, b + 1, buffers["passed"])
    pool.indirect_dma_start(out=buffers[which + "_raw"][i][:, :], out_offset=None, in_=dram[which],
                            in_offset=bass.IndirectOffsetOnAxis(ap=index[:, :], axis=0)).then_inc(buffers[which + "_ld"][i], 16)


def route_phase(nc, layer, shared, dram, buffers):
    x, ident = shared["x"], shared["ident"]
    tg = shared["tanh_g"][:, 2 + layer:3 + layer]

    with ExitStack() as ctx:
        def sb(name, shape, dt=F32):
            return ctx.enter_context(nc.sbuf_tensor(f"{name}_r{layer}", shape, dt))

        def ps(name, shape):
            return ctx.enter_context(nc.psum_tensor(f"{name}_r{layer}", shape, F32))

        new_sem = semaphores(nc, ctx)

        def sem(name):
            return new_sem(f"{name}_r{layer}")

        gate_w = sb("gate_w", [P, KC, E])
        gate_b = sb("gate_b", [P, E])
        xn = sb("xn", [P, TT, D])
        stats, mean_var = sb("stats", [P, TT, 6]), sb("mean_var", [P, TT, 2])
        var_eps, rstd, minus_half = sb("var_eps", [P, TT]), sb("rstd", [P, TT]), sb("minus_half", [P, TT])
        xt = [sb(f"xt{i}", [P, KC, P]) for i in range(2)]
        exp_no, exp_rank, blk_no, row_no = sb("exp_no", [P, E]), sb("exp_rank", [P, E]), sb("blk_no", [P, L0_BLOCKS]), sb("row_no", [P, 1])
        score, score2, tmp = sb("score", [P, TT, E]), sb("score2", [P, TT, E]), sb("tmp", [P, TT, E])
        shifted, expo = sb("shifted", [P, TT, E]), sb("expo", [P, TT, E])
        top = [sb(f"top{i}", [P, TT]) for i in range(2)]
        col = [sb(f"col{i}", [P, TT]) for i in range(2)]
        one_hot = [sb(f"one_hot{i}", [P, TT, E]) for i in range(2)]
        chosen = sb("chosen", [P, TT, E], BF16)
        wt = [sb(f"wt{i}", [P, TT]) for i in range(2)]
        diff, ratio, den = sb("diff", [P, TT]), sb("ratio", [P, TT]), sb("den", [P, TT])
        count, blocks_i, blocks_f = sb("count", [P, E], I32), sb("blocks_i", [P, E], I32), sb("blocks_f", [P, E])
        earlier, first, end = sb("earlier", [P, E, E]), sb("first", [P, E]), sb("end", [P, E])
        base, place, valid = sb("base", [P, E]), sb("place", [P, TT, E]), sb("valid", [P, TT, E])
        past, blk_row, blk_expert = sb("past", [P, L0_BLOCKS, E]), sb("blk_row", [P, L0_BLOCKS]), sb("blk_expert", [P, L0_BLOCKS])
        lane_no, half_no, token_no = sb("lane_no", [P, P]), sb("half_no", [P, HALVES]), sb("token_no", [P, TT])
        quotient, remainder = sb("quotient", [P, 2, TT], I32), sb("remainder", [P, 2, TT], I32)
        half_of, lane_of = sb("half_of", [P, 2, TT]), sb("lane_of", [P, 2, TT])
        is_half = sb("is_half", [P, TT, HALVES], F16)
        token_at = [sb(f"token_at{i}", [P, TT, HALVES], F16) for i in range(2)]
        is_lane = [sb(f"is_lane{i}", [P, TT, P], F16) for i in range(2)]
        noop = [sb(f"noop{i}", [P, TT]) for i in range(2)]

        ps_xt = [ps(f"ps_xt{i}", [P, KC, P]) for i in range(2)]
        ps_lg = ps("ps_lg", [P, TT, E])
        ps_rank = ps("ps_rank", [P, TT, E])
        ps_cnt = ps("ps_cnt", [P, E])
        ps_token = ps("ps_token", [P, HALVES])

        g_ld, const, ln_stats, ln_mean, ln_eps, ln_rstd, xn_ready, xt_ps, xt_ready, lg_ps = (
            sem(n) for n in ("g_ld", "const", "ln_stats", "ln_mean", "ln_eps", "ln_rstd", "xn_ready", "xt_ps",
                             "xt_ready", "lg_ps"))
        step, exp_in, exp_done, chosen_ready, rank_ps, slots_ready, stored, tables_ready, token_ps, blocks_ready = (
            sem(n) for n in ("step", "exp_in", "exp_done", "chosen_ready", "rank_ps", "slots_ready", "stored", "tables_ready",
                             "token_ps", "blocks_ready"))
        block = ctx.enter_context(nc.Block())

        @block.sync
        def _(sp):
            if layer:
                for n, b in (("w1", 0), ("w2", 0), ("w1", 1)):
                    sp.dma_start(buffers[n + "_raw"][b][:, :], dram[n][b * P:b * P + P, :]).then_inc(buffers[n + "_ld"][b], 16)
            sp.dma_start(gate_w[:, :, :], dram["gate_w"].rearrange("(k p) e -> p k e", p=P)).then_inc(g_ld, 16)
            if layer:
                sp.dma_start(gate_b[:, :], dram["gate_b"]).then_inc(g_ld, 16)
            dst = dram["xn"].rearrange("(t p) d -> p t d", p=P)
            for c in range(TT // CT):
                sp.wait_ge(xn_ready, c * CT + CT)
                sp.dma_start(dst[:, c * CT:(c + 1) * CT, :], xn[:, c * CT:(c + 1) * CT, :]).then_inc(stored, 16)
            sp.wait_ge(stored, 16 * (TT // CT))

        @block.gpsimd
        def _(pool):
            pool.memset(minus_half[:, :], -0.5).then_inc(const, 1)
            pool.wait_ge(const, 1)
            for c in range(TT // CT):
                tiles = slice(c * CT, c * CT + CT)
                pool.wait_ge(ln_mean, c * CT + CT)
                pool.tensor_scalar(var_eps[:, tiles], mean_var[:, tiles, 1], EPS, None, ALU.add).then_inc(ln_eps, 1)
                pool.wait_ge(ln_eps, c + 1)
                pool.tensor_tensor(rstd[:, tiles], var_eps[:, tiles], minus_half[:, tiles], ALU.pow).then_inc(ln_rstd, 1)
            if layer == 0:
                pool.wait_ge(blocks_ready, 1)
                for n, b in (("w1", 0), ("w2", 0), ("w1", 1)):
                    gather_weights(pool, n, buffers, shared, dram, b, b)

        @block.scalar
        def _(act):
            with act.Fori(0, TT // 2) as t:
                for i in range(2):
                    act.wait_ge(xt_ps, t * 2 + i + 1)
                    act.activation(xt[i][:, :, :], ps_xt[i][:, :, :], ACT.Copy).then_inc(xt_ready, 1)
            act.wait_ge(exp_in, 1)
            if layer == 0:
                act.activation(ratio[:, :], diff[:, :], ACT.Exp).then_inc(exp_done, 1)
            else:
                act.activation(expo[:, :, :], shifted[:, :, :], ACT.Exp).then_inc(exp_done, 1)

        @block.tensor
        def _(pe):
            def turn(t, i):
                pe.wait_ge(xn_ready, t + 1)
                for k in range(KC):
                    ins = pe.transpose(ps_xt[i][:, k, :], xn[:, t, k * P:(k + 1) * P], ident[:, :])
                ins.then_inc(xt_ps, 1)

            def logits(t, i):
                pe.wait_ge(xt_ready, t + 1)
                for k in range(KC):
                    ins = pe.matmul(ps_lg[:, t, :], xt[i][:, k, :], gate_w[:, k, :],
                                    start=k == 0, stop=k == KC - 1)
                ins.then_inc(lg_ps, 1)

            pe.wait_ge(g_ld, 16 + 16 * layer)
            turn(0, 0)
            for t in range(1, TT):
                turn(t, t % 2)
                logits(t - 1, 1 - t % 2)
            logits(TT - 1, (TT - 1) % 2)
            pe.wait_ge(chosen_ready, 1)
            pe.matmul(ps_rank[:, :, :], shared["before"][:, :], chosen[:, :, :], start=True, stop=False)
            for s in range(TT - 1):
                pe.matmul(ps_rank[:, s + 1:TT, :], shared["ones"][:, :], spread(chosen[:, s, :], 1, TT - 1 - s),
                          start=False, stop=s == TT - 2)
            for s in range(TT):
                ins = pe.matmul(ps_cnt[:, :], shared["ones"][:, :], chosen[:, s, :], start=s == 0, stop=s == TT - 1)
            ins.then_inc(rank_ps, 1)
            for i in range(2):
                pe.wait_ge(tables_ready, i + 1)
                for t in range(TT):
                    ins = pe.matmul(ps_token[:, :], is_lane[i][:, t, :], token_at[i][:, t, :], start=i == 0 and t == 0,
                                    stop=i == 1 and t == TT - 1)
            ins.then_inc(token_ps, 1)

        @block.vector
        def _(dve):
            dve.tensor_copy(exp_no[:, :], shared["expert_no"][:, :]).then_inc(const, 1)
            dve.tensor_copy(blk_no[:, :], shared["block_no"][:, :]).then_inc(const, 1)
            dve.tensor_copy(row_no[:, :], shared["row_no"][:, :]).then_inc(const, 1)
            dve.tensor_copy(lane_no[:, :], shared["lane_no"][:, :]).then_inc(const, 1)
            dve.tensor_copy(half_no[:, :], shared["lane_no"][:, 0:HALVES]).then_inc(const, 1)
            dve.tensor_copy(token_no[:, :], shared["token_no"][:, :]).then_inc(const, 1)
            dve.wait_ge(const, 7)
            dve.tensor_scalar(exp_rank[:, :], exp_no[:, :], -1.0, float(E), ALU.mult, ALU.add).then_inc(const, 1)
            dve.tensor_tensor(earlier[:, :, :], spread(exp_no[:, :], 1, E), spread(exp_no[:, :], 2, E),
                              ALU.is_lt).then_inc(const, 1)
            dve.wait_ge(const, 9)

            def moments(c):
                for t in range(c * CT, c * CT + CT):
                    dve.bn_stats(stats[:, t, :], x[:, t, :]).then_inc(ln_stats, 1)
                for t in range(c * CT, c * CT + CT):
                    dve.wait_ge(ln_stats, t + 1)
                    dve.bn_aggr(mean_var[:, t, :], stats[:, t, :]).then_inc(ln_mean, 1)

            def normalise(c):
                dve.wait_ge(ln_rstd, c + 1)
                for t in range(c * CT, c * CT + CT):
                    dve.tensor_scalar(xn[:, t, :], x[:, t, :], mean_var[:, t, 0:1], rstd[:, t:t + 1], ALU.subtract,
                                      ALU.mult).then_inc(xn_ready, 1)

            moments(0)
            for c in range(1, TT // CT):
                moments(c)
                normalise(c - 1)
            normalise(TT // CT - 1)

            dve.wait_ge(lg_ps, TT)
            if layer == 0:
                dve.tensor_copy(score[:, :, :], ps_lg[:, :, :]).then_inc(step, 1)
                dve.wait_ge(step, 1)
            else:
                dve.wait_ge(g_ld, 32)
                dve.tensor_tensor(tmp[:, :, :], ps_lg[:, :, :], spread(gate_b[:, :], 1, TT), ALU.add).then_inc(step, 1)
                dve.wait_ge(step, 1)
                dve.tensor_reduce(den[:, :], tmp[:, :, :], AX.X, ALU.max).then_inc(step, 1)
                dve.wait_ge(step, 2)
                dve.tensor_tensor(shifted[:, :, :], tmp[:, :, :], spread(den[:, :], 2, E), ALU.subtract).then_inc(exp_in, 1)
                dve.wait_ge(exp_done, 1)
                dve.tensor_reduce(diff[:, :], expo[:, :, :], AX.X, ALU.add).then_inc(step, 1)
                dve.wait_ge(step, 3)
                dve.reciprocal(ratio[:, :], diff[:, :]).then_inc(step, 1)
                dve.wait_ge(step, 4)
                dve.tensor_tensor(score[:, :, :], expo[:, :, :], spread(ratio[:, :], 2, E), ALU.mult).then_inc(step, 1)
                dve.wait_ge(step, 5)
            n = 5 if layer else 1

            for i in range(2):
                src = score2 if i else score
                if i:
                    dve.scalar_tensor_tensor(score2[:, :, :], one_hot[0][:, :, :], -3e38, score[:, :, :], ALU.mult,
                                             ALU.add).then_inc(step, 1)
                    dve.wait_ge(step, n + 5)
                m = n + 5 * i
                dve.tensor_reduce(top[i][:, :], src[:, :, :], AX.X, ALU.max).then_inc(step, 1)
                dve.wait_ge(step, m + 1)
                dve.tensor_tensor(tmp[:, :, :], src[:, :, :], spread(top[i][:, :], 2, E), ALU.is_equal).then_inc(step, 1)
                dve.wait_ge(step, m + 2)
                dve.tensor_tensor(valid[:, :, :], tmp[:, :, :], spread(exp_rank[:, :], 1, TT), ALU.mult).then_inc(step, 1)
                dve.wait_ge(step, m + 3)
                dve.tensor_reduce(col[i][:, :], valid[:, :, :], AX.X, ALU.max).then_inc(step, 1)
                dve.wait_ge(step, m + 4)
                dve.tensor_tensor(one_hot[i][:, :, :], spread(exp_rank[:, :], 1, TT), spread(col[i][:, :], 2, E),
                                  ALU.is_equal).then_inc(step, 1)
                if i == 0:
                    dve.wait_ge(step, m + 5)
                    n += 1
            n += 10
            dve.wait_ge(step, n)

            if layer == 1:
                for i in range(2):
                    dve.tensor_scalar(col[i][:, :], top[i][:, :], 0.0, None, ALU.is_gt).then_inc(step, 1)
                    dve.wait_ge(step, n + 2 * i + 1)
                    dve.tensor_tensor(one_hot[i][:, :, :], one_hot[i][:, :, :], spread(col[i][:, :], 2, E),
                                      ALU.mult).then_inc(step, 1)
                    dve.wait_ge(step, n + 2 * i + 2)
                n += 4
            dve.tensor_tensor(chosen[:, :, :], one_hot[0][:, :, :], one_hot[1][:, :, :], ALU.add).then_inc(chosen_ready, 1)

            if layer == 0:
                dve.tensor_tensor(diff[:, :], top[1][:, :], top[0][:, :], ALU.subtract).then_inc(exp_in, 1)
                dve.wait_ge(exp_done, 1)
                dve.tensor_scalar(den[:, :], ratio[:, :], 1.0, None, ALU.add).then_inc(step, 1)
                dve.wait_ge(step, n + 1)
                dve.reciprocal(wt[0][:, :], den[:, :]).then_inc(step, 1)
                dve.wait_ge(step, n + 2)
                dve.tensor_tensor(wt[1][:, :], ratio[:, :], wt[0][:, :], ALU.mult).then_inc(step, 1)
                dve.wait_ge(step, n + 3)
                n += 3
            weights = top if layer else wt
            for i in range(2):
                dve.tensor_scalar(shared["weight"][i][:, :], weights[i][:, :], tg, None, ALU.mult).then_inc(step, 1)
            n += 2
            dve.wait_ge(step, n)

            dve.wait_ge(rank_ps, 1)
            if layer == 0:
                dve.tensor_scalar(count[:, :], ps_cnt[:, :], float(SB - 1), None, ALU.add).then_inc(step, 1)
                dve.wait_ge(step, n + 1)
                dve.tensor_scalar(blocks_i[:, :], count[:, :], SB.bit_length() - 1, None,
                                  ALU.arith_shift_right).then_inc(step, 1)
                dve.wait_ge(step, n + 2)
                dve.tensor_copy(blocks_f[:, :], blocks_i[:, :]).then_inc(step, 1)
                dve.wait_ge(step, n + 3)
                dve.tensor_tensor(earlier[:, :, :], earlier[:, :, :], spread(blocks_f[:, :], 1, E), ALU.mult).then_inc(step, 1)
                dve.wait_ge(step, n + 4)
                dve.tensor_reduce(first[:, :], earlier[:, :, :], AX.X, ALU.add).then_inc(step, 1)
                dve.wait_ge(step, n + 5)
                dve.tensor_scalar(base[:, :], first[:, :], float(SB), float(-SLOTS), ALU.mult, ALU.add).then_inc(step, 1)
                dve.tensor_tensor(end[:, :], first[:, :], blocks_f[:, :], ALU.add).then_inc(step, 1)
                dve.wait_ge(step, n + 7)
                n += 7
                dve.tensor_tensor(place[:, :, :], ps_rank[:, :, :], spread(base[:, :], 1, TT), ALU.add).then_inc(step, 1)
                dve.tensor_tensor(past[:, :, :], spread(end[:, :], 1, L0_BLOCKS), spread(blk_no[:, :], 2, E),
                                  ALU.is_le).then_inc(step, 1)
                dve.wait_ge(step, n + 2)
                dve.tensor_reduce(blk_expert[:, :], past[:, :, :], AX.X, ALU.add).then_inc(step, 1)
                dve.wait_ge(step, n + 3)
                dve.tensor_scalar(blk_row[:, :], blk_expert[:, :], float(E - 1), float(P), ALU.min, ALU.mult).then_inc(step, 1)
                dve.wait_ge(step, n + 4)
                dve.tensor_scalar(shared["block_row"][:, :], blk_row[:, :], row_no[:, 0:1], None, ALU.add).then_inc(blocks_ready, 1)
                n += 4
            else:
                dve.tensor_scalar(base[:, :], exp_no[:, :], float(SB), float(-SLOTS), ALU.mult, ALU.add).then_inc(step, 1)
                dve.tensor_scalar(valid[:, :, :], ps_rank[:, :, :], float(SB), None, ALU.is_lt).then_inc(step, 1)
                dve.tensor_scalar(first[:, :], exp_no[:, :], float(E - 1), None, ALU.is_lt).then_inc(step, 1)
                dve.wait_ge(step, n + 3)
                dve.tensor_tensor(tmp[:, :, :], ps_rank[:, :, :], spread(base[:, :], 1, TT), ALU.add).then_inc(step, 1)
                dve.tensor_tensor(valid[:, :, :], valid[:, :, :], spread(first[:, :], 1, TT), ALU.mult).then_inc(step, 1)
                dve.wait_ge(step, n + 5)
                dve.tensor_tensor(place[:, :, :], tmp[:, :, :], valid[:, :, :], ALU.mult).then_inc(step, 1)
                n += 6
            dve.wait_ge(step, n)
            for i in range(2):
                dve.tensor_tensor(tmp[:, :, :], one_hot[i][:, :, :], place[:, :, :], ALU.mult).then_inc(step, 1)
                dve.wait_ge(step, n + 3 * i + 1)
                dve.tensor_reduce(col[i][:, :], tmp[:, :, :], AX.X, ALU.add).then_inc(step, 1)
                dve.wait_ge(step, n + 3 * i + 2)
                dve.tensor_scalar(shared["slot"][i][:, :], col[i][:, :], float(SLOTS), None, ALU.add).then_inc(slots_ready, 1)
                if i == 0:
                    dve.sem_inc(step, 1)
            n += 5
            dve.wait_ge(slots_ready, 2)

            for i in range(2):
                dve.tensor_scalar(quotient[:, i, :], shared["slot"][i][:, :], P.bit_length() - 1, None,
                                  ALU.arith_shift_right).then_inc(step, 1)
                dve.tensor_scalar(remainder[:, i, :], shared["slot"][i][:, :], P - 1, None,
                                  ALU.bitwise_and).then_inc(step, 1)
            dve.wait_ge(step, n + 4)
            dve.tensor_copy(half_of[:, :, :], quotient[:, :, :]).then_inc(step, 1)
            dve.tensor_copy(lane_of[:, :, :], remainder[:, :, :]).then_inc(step, 1)
            dve.wait_ge(step, n + 6)
            n += 6
            for i in range(2):
                if i:
                    dve.wait_ge(tables_ready, i)
                dve.tensor_tensor(is_half[:, :, :], spread(half_no[:, :], 1, TT), spread(half_of[:, i, :], 2, HALVES),
                                  ALU.is_equal).then_inc(step, 1)
                dve.tensor_tensor(is_lane[i][:, :, :], spread(lane_no[:, :], 1, TT), spread(lane_of[:, i, :], 2, P),
                                  ALU.is_equal).then_inc(step, 1)
                dve.wait_ge(step, n + 2)
                n += 2
                dve.tensor_tensor(token_at[i][:, :, :], is_half[:, :, :], spread(token_no[:, :], 2, HALVES),
                                  ALU.mult).then_inc(tables_ready, 1)

            if layer == 1:
                for i in range(2):
                    dve.tensor_tensor(noop[i][:, :], one_hot[i][:, :, E - 1], shared["weight"][i][:, :], ALU.mult).then_inc(step, 1)
                dve.wait_ge(step, n + 2)
                dve.tensor_tensor(shared["noop"][:, :], noop[0][:, :], noop[1][:, :], ALU.add).then_inc(step, 1)
                n += 3
            dve.wait_ge(step, n)
            dve.wait_ge(token_ps, 1)
            dve.tensor_copy(shared["token_of"][:, :], ps_token[:, :]).then_inc(step, 1)
            dve.wait_ge(step, n + 1)


def expert_phase(nc, layer, shared, dram, buffers):
    ident = shared["ident"]
    blocks = E - 1 if layer else L0_BLOCKS
    RB = 4

    with ExitStack() as ctx:
        def sb(name, shape, dt=F32):
            return ctx.enter_context(nc.sbuf_tensor(f"{name}_e{layer}", shape, dt))

        def ps(name, shape):
            return ctx.enter_context(nc.psum_tensor(f"{name}_e{layer}", shape, F32))

        new_sem = semaphores(nc, ctx)

        def sem(name):
            return new_sem(f"{name}_e{layer}")

        w1_raw, w2_raw, w1_ld, w2_ld = (buffers[n] for n in ("w1_raw", "w2_raw", "w1_ld", "w2_ld"))
        w1 = [[sb(f"w1_{i}{j}", [P, KC, FC, P], F32R) for j in range(2)] for i in range(2)]
        w2 = [[sb(f"w2_{i}{j}", [P, FC, D], F32R) for j in range(2)] for i in range(2)]
        b1 = [sb(f"b1_{i}", [P, FC]) for i in range(2)]
        b2 = [sb(f"b2_{i}", [P, D]) for i in range(2)]
        xe = [sb(f"xe{i}", [P, QT, D]) for i in range(2)]
        xe_t = [[sb(f"xe_t{i}{j}", [P, KC, SB], F32R) for j in range(2)] for i in range(2)]
        hid = [sb(f"hid{i}", [P, 2, SB]) for i in range(2)]
        h = [[sb(f"h{i}{j}", [P, FC, SB], F32R) for j in range(2)] for i in range(2)]
        y = [sb(f"y{i}", [P, QT, D]) for i in range(2)]

        ps_x = [ps(f"ps_x{i}", [P, KC, SB]) for i in range(2)]
        ps_h = [ps(f"ps_h{i}", [P, 2, SB]) for i in range(RB)]
        ps_y = [ps(f"ps_y{i}", [P, QT, D]) for i in range(2)]

        xe_ld, stored = ([sem(f"{n}{i}") for i in range(2)] for n in ("xe_ld", "stored"))
        w1_hi, w1_ready, w2_hi, w2_ready, xe_ps, xe_hi, xe_ready, h_ps, hid_ready, h_hi, h_ready, y_ps, y_ready = (
            sem(n) for n in ("w1_hi", "w1_ready", "w2_hi", "w2_ready", "xe_ps", "xe_hi", "xe_ready", "h_ps",
                             "hid_ready", "h_hi", "h_ready", "y_ps", "y_ready"))
        xe_indexed = sem("xe_indexed")
        xe_index = [sb(f"xe_index{i}", [P, QT], I32) for i in range(2)]
        passed = sem("passed")
        NP = FC // 2

        block = ctx.enter_context(nc.Block())
        ye_dst = dram["ye"][0:SLOTS, :].rearrange("(b q p) d -> p b q d", p=P, q=QT)

        def one(ap, b):
            return ap[:, bass.ds(b, 1), :, :].rearrange("p b q d -> p (b q) d")

        @block.sync
        def _(sp):
            def body(b, i, w1_more=True, w2_more=True, first=False):
                if layer:
                    if w1_more:
                        sp.wait_ge(w1_ready, b + 1)
                        sp.dma_start(w1_raw[i][:, :], dram["w1"][bass.ds((b + 2) * P, P), :]).then_inc(w1_ld[i], 16)
                    if w2_more:
                        if not first:
                            sp.wait_ge(w2_ready, b)
                        sp.dma_start(w2_raw[1 - i][:, :], dram["w2"][bass.ds((b + 1) * P, P), :]).then_inc(w2_ld[1 - i], 16)
                if not first:
                    sp.wait_ge(y_ready, b)
                    sp.dma_start(one(ye_dst, b - 1), y[1 - i][:, :, :]).then_inc(stored[1 - i], 16)

            body(0, 0, first=True)
            with sp.Fori(0, (blocks - 3) // 2) as t:
                body(t * 2 + 1, 1)
                body(t * 2 + 2, 0)
            for b in range((blocks - 3) // 2 * 2 + 1, blocks + 1):
                body(b, b % 2, w1_more=b + 2 < blocks, w2_more=b + 1 < blocks)
            for i in range(2):
                sp.wait_ge(stored[i], 16 * ((blocks - i + 1) // 2))

        @block.gpsimd
        def _(pool):
            def load_w1(b, i):
                if layer == 0:
                    gather_weights(pool, "w1", buffers, shared, dram, b, i)

            def load_w2(b, i):
                if layer == 0:
                    gather_weights(pool, "w2", buffers, shared, dram, b, i)

            def load_x(b, i):
                pool.tensor_copy(xe_index[i][:, :], shared["token_of"][:, bass.ds(b * QT, QT)]).then_inc(xe_indexed, 1)
                wait_apart(pool, xe_indexed, b + 1, passed)
                for q in range(QT):
                    pool.indirect_dma_start(
                        out=xe[i][:, q, :], out_offset=None, in_=dram["xn"],
                        in_offset=bass.IndirectOffsetOnAxis(ap=xe_index[i][:, q:q + 1], axis=0)).then_inc(xe_ld[i], 16)

            def body(b, i, first=False, w1_more=True, w2_more=True):
                if w1_more:
                    if layer == 0:
                        wait_apart(pool, w1_ready, b + 1, passed)
                        load_w1(b + 2, i)
                if w2_more:
                    if not first and layer == 0:
                        wait_apart(pool, w2_ready, b, passed)
                    load_w2(b + 1, 1 - i)
                if w1_more:
                    wait_apart(pool, xe_ps, b + 1, passed)
                    load_x(b + 2, i)

            load_x(0, 0)
            load_x(1, 1)
            body(0, 0, first=True)
            with pool.Fori(0, (blocks - 3) // 2) as t:
                body(t * 2 + 1, 1)
                body(t * 2 + 2, 0)
            for b in range((blocks - 3) // 2 * 2 + 1, blocks):
                body(b, b % 2, w1_more=b + 2 < blocks, w2_more=b + 1 < blocks)

        def w1_view(raw, k):
            return raw[:, k * F:(k + 1) * F].rearrange("p (f j) -> p j f", j=FC)

        @block.scalar
        def _(act):
            def w1_high(b, i, half, k):
                if k == 0:
                    act.wait_ge(w1_ld[i], (half + 1) * 16)
                    wait(act, h_ps, (b - 1) * NP)
                act.activation(w1[i][0][:, k, :, :], w1_view(w1_raw[i], k), ACT.Copy).then_inc(w1_hi, 1)

            def w2_high(b, i, half, k):
                if k == 0:
                    act.wait_ge(w2_ld[i], (half + 1) * 16)
                    wait(act, y_ps, b - 1)
                js = slice(k * FC // 2, (k + 1) * FC // 2)
                act.activation(w2[i][0][:, js, :], w2_raw[i][:, 0:FC * D].rearrange("p (j d) -> p j d", d=D)[:, js, :],
                               ACT.Copy).then_inc(w2_hi, 1)

            def hidden(b, i, half, jp):
                act.wait_ge(h_ps, b * NP + jp + 1)
                wait(act, h_ready, b * NP + jp - 1)
                if layer:
                    act.activation(hid[jp % 2][:, :, :], ps_h[jp % RB][:, :, :], ACT.Relu).then_inc(hid_ready, 1)
                else:
                    for j in range(2):
                        ins = act.activation(hid[jp % 2][:, j, :], ps_h[jp % RB][:, j, :], ACT.Gelu,
                                             bias=b1[i][:, 2 * jp + j:2 * jp + j + 1])
                    ins.then_inc(hid_ready, 1)

            def inputs_high(b, i):
                act.wait_ge(xe_ps, b + 1)
                act.activation(xe_t[i][0][:, :, :], ps_x[i][:, :, :], ACT.Copy).then_inc(xe_hi, 1)

            def body(b, i, half, more=True):
                for jp in range(NP):
                    if jp < KC:
                        if more:
                            w1_high(b + 1, 1 - i, half + i, jp)
                    else:
                        w2_high(b, i, half, jp - KC)
                    if jp == NP - 1 and more:
                        inputs_high(b + 1, 1 - i)
                    hidden(b, i, half, jp)

            for k in range(KC):
                w1_high(0, 0, 0, k)
            inputs_high(0, 0)
            body(0, 0, 0)
            with act.Fori(0, (blocks - 2) // 2) as t:
                body(t * 2 + 1, 1, t)
                body(t * 2 + 2, 0, t + 1)
            for b in range((blocks - 2) // 2 * 2 + 1, blocks):
                body(b, b % 2, b // 2, more=b + 1 < blocks)

        @block.vector
        def _(dve):
            def w1_low(b, i, k):
                dve.wait_ge(w1_hi, b * KC + k + 1)
                ins = dve.tensor_tensor(w1[i][1][:, k, :, :], w1_view(w1_raw[i], k), w1[i][0][:, k, :, :].bitcast(F32),
                                        ALU.subtract)
                if k == KC - 1:
                    if layer == 0:
                        ins = dve.tensor_copy(b1[i][:, :], w1_raw[i][:, KC * F:KC * F + FC])
                    ins.then_inc(w1_ready, 1)

            def w2_low(b, i, k):
                dve.wait_ge(w2_hi, b * 2 + k + 1)
                js = slice(k * FC // 2, (k + 1) * FC // 2)
                ins = dve.tensor_tensor(w2[i][1][:, js, :], w2_raw[i][:, 0:FC * D].rearrange("p (j d) -> p j d", d=D)[:, js, :],
                                        w2[i][0][:, js, :].bitcast(F32), ALU.subtract)
                if k == 1:
                    if layer == 0:
                        ins = dve.tensor_copy(b2[i][:, :], w2_raw[i][:, FC * D:FC * D + D])
                    ins.then_inc(w2_ready, 1)

            def hidden_parts(b, i, jp):
                js = slice(2 * jp, 2 * jp + 2)
                dve.wait_ge(hid_ready, b * NP + jp + 1)
                wait(dve, y_ps, b - 1)
                dve.tensor_copy(h[i][0][:, js, :], hid[jp % 2][:, :, :]).then_inc(h_hi, 1)
                dve.wait_ge(h_hi, b * NP + jp + 1)
                dve.tensor_tensor(h[i][1][:, js, :], hid[jp % 2][:, :, :], h[i][0][:, js, :].bitcast(F32),
                                  ALU.subtract).then_inc(h_ready, 1)

            def output(b, i, half):
                dve.wait_ge(y_ps, b + 1)
                wait(dve, stored[i], half * 16)
                if layer:
                    dve.tensor_copy(y[i][:, :, :], ps_y[i][:, :, :]).then_inc(y_ready, 1)
                else:
                    dve.tensor_tensor(y[i][:, :, :], ps_y[i][:, :, :], spread(b2[i][:, :], 1, QT), ALU.add).then_inc(y_ready, 1)

            def inputs_low(b, i):
                dve.wait_ge(xe_hi, b + 1)
                dve.tensor_tensor(xe_t[i][1][:, :, :], ps_x[i][:, :, :], xe_t[i][0][:, :, :].bitcast(F32),
                                  ALU.subtract).then_inc(xe_ready, 1)

            def body(b, i, half, first=False, more=True):
                for jp in range(NP):
                    if jp < KC:
                        if more:
                            w1_low(b + 1, 1 - i, jp)
                    else:
                        w2_low(b, i, jp - KC)
                    if jp == NP - 1 and more:
                        inputs_low(b + 1, 1 - i)
                    hidden_parts(b, i, jp)
                if not first:
                    output(b - 1, 1 - i, half - 1 + i)

            for k in range(KC):
                w1_low(0, 0, k)
            inputs_low(0, 0)
            body(0, 0, 0, first=True)
            with dve.Fori(0, (blocks - 2) // 2) as t:
                body(t * 2 + 1, 1, t)
                body(t * 2 + 2, 0, t + 1)
            for b in range((blocks - 2) // 2 * 2 + 1, blocks):
                body(b, b % 2, b // 2, more=b + 1 < blocks)
            output(blocks - 1, (blocks - 1) % 2, (blocks - 1) // 2)

        @block.tensor
        def _(pe):
            def turn(b, i, half):
                pe.wait_ge(xe_ld[i], (half + 1) * 16 * QT)
                wait(pe, xe_ready, b - 1)
                for q in range(QT):
                    rows = xe[i][:, q, :].rearrange("p (d k) -> p k d", k=KC)
                    for k in range(KC):
                        ins = pe.transpose(ps_x[i][:, k, q * P:(q + 1) * P], rows[:, k, :], ident[:, :])
                ins.then_inc(xe_ps, 1)

            def first_product(b, i, more, half):
                pe.wait_ge(xe_ready, b + 1)
                pe.wait_ge(w1_ready, b + 1)
                for jp in range(NP):
                    wait(pe, hid_ready, b * NP + jp + 1 - RB)
                    for j in range(2):
                        for k in range(KC):
                            ins = split_matmul(pe, ps_h[jp % RB][:, j, :], [w1[i][s][:, k, 2 * jp + j, :] for s in range(2)],
                                               [xe_t[i][s][:, k, :] for s in range(2)], k == 0, k == KC - 1)
                    ins.then_inc(h_ps, 1)
                    if jp == NP - 2 and more:
                        turn(b + 1, 1 - i, half + i)

            def second_product(b, i):
                pe.wait_ge(w2_ready, b + 1)
                pe.wait_ge(h_ready, (b + 1) * NP)
                wait(pe, y_ready, b - 1)
                for q in range(QT):
                    for j in range(FC):
                        ins = split_matmul(pe, ps_y[i][:, q, :], [h[i][s][:, j, q * P:(q + 1) * P] for s in range(2)],
                                           [w2[i][s][:, j, :] for s in range(2)], j == 0, j == FC - 1)
                ins.then_inc(y_ps, 1)

            def body(b, i, half, more=True):
                first_product(b, i, more, half)
                second_product(b - 1, 1 - i)

            turn(0, 0, 0)
            first_product(0, 0, True, 0)
            body(1, 1, 0)
            with pe.Fori(1, blocks // 2) as t:
                body(t * 2, 0, t)
                body(t * 2 + 1, 1, t)
            for b in range(blocks // 2 * 2, blocks):
                body(b, b % 2, b // 2, more=b + 1 < blocks)
            second_product(blocks - 1, (blocks - 1) % 2)


def combine_phase(nc, shared, dram):
    x = shared["x"]
    RY = 4
    with ExitStack() as ctx:
        rows = [[ctx.enter_context(nc.sbuf_tensor(f"rows{r}{i}_c", [P, D], F32)) for i in range(2)] for r in range(RY)]
        sem = semaphores(nc, ctx)
        rows_ld = [sem(f"rows_ld{r}_c") for r in range(RY)]
        xn = ctx.enter_context(nc.sbuf_tensor("xn_c", [P, TT, D], F32))
        xn_ld, noop_added = sem("xn_ld_c"), sem("noop_added_c")
        passed = sem("passed_c")
        added = sem("added_c")
        half_added = sem("half_added_c")
        stored = sem("out_stored_c")
        block = ctx.enter_context(nc.Block())

        @block.gpsimd
        def _(pool):
            def gather(t, r):
                for i in range(2):
                    pool.indirect_dma_start(
                        out=rows[r][i][:, :], out_offset=None, in_=dram["ye"],
                        in_offset=bass.IndirectOffsetOnAxis(ap=shared["slot"][i][:, t:t + 1], axis=0)).then_inc(rows_ld[r], 16)

            pool.wait_ge(shared["cleared"], 16)
            for t in range(TT):
                wait(pool, added, t - RY + 1)
                gather(t, t % RY)

        @block.vector
        def _(dve):
            dve.wait_ge(xn_ld, 16)
            with dve.Fori(0, TT // RY) as u:
                for r in range(RY):
                    xt = x[:, bass.ds(u * RY + r, 1), :].rearrange("p t d -> p (t d)")
                    dve.scalar_tensor_tensor(xt, xn[:, bass.ds(u * RY + r, 1), :].rearrange("p t d -> p (t d)"),
                                             shared["noop"][:, bass.ds(u * RY + r, 1)], xt, ALU.mult,
                                             ALU.add).then_inc(noop_added, 1)
                    wait_apart(dve, noop_added, u * RY + r + 1, passed)
                    dve.wait_ge(rows_ld[r], (u + 1) * 32)
                    dve.scalar_tensor_tensor(xt, rows[r][0][:, :], shared["weight"][0][:, bass.ds(u * RY + r, 1)], xt,
                                             ALU.mult, ALU.add).then_inc(half_added, 1)
                    dve.wait_ge(half_added, u * RY + r + 1)
                    dve.scalar_tensor_tensor(xt, rows[r][1][:, :], shared["weight"][1][:, bass.ds(u * RY + r, 1)], xt,
                                             ALU.mult, ALU.add).then_inc(added, 1)
            dve.wait_ge(added, TT)

        @block.sync
        def _(sp):
            sp.dma_start(xn[:, :, :], dram["xn"].rearrange("(t p) d -> p t d", p=P)).then_inc(xn_ld, 16)
            dst = dram["out"].rearrange("(t p) d -> p t d", p=P)
            for u in range(TT // RY):
                tiles = slice(u * RY, u * RY + RY)
                sp.wait_ge(added, (u + 1) * RY)
                sp.dma_start(dst[:, tiles, :], x[:, tiles, :]).then_inc(stored, 16)
            sp.wait_ge(stored, 16 * (TT // RY))


def program(nc, dram):
    with ExitStack() as ctx:
        def sb(name, shape, dt=F32):
            return ctx.enter_context(nc.sbuf_tensor(name, shape, dt))

        shared = {
            "x": sb("x_sb", [P, TT, D]),
            "ident": sb("ident", [P, P]),
            "zeros": sb("zeros", [P, D]),
            "ones": sb("ones", [P, P], BF16),
            "before": sb("before", [P, P], BF16),
            "expert_no": sb("expert_no", [P, E], I32),
            "block_no": sb("block_no", [P, L0_BLOCKS], I32),
            "lane_no": sb("lane_no_i", [P, P], I32),
            "token_no": sb("token_no_i", [P, TT], I32),
            "token_of": sb("token_of", [P, HALVES], I32),
            "row_no": sb("row_no_i", [P, 1], I32),
            "tanh_g": sb("tanh_g", [P, 4]),
            "slot": [sb(f"slot{i}", [P, TT], I32) for i in range(2)],
            "weight": [sb(f"weight{i}", [P, TT]) for i in range(2)],
            "noop": sb("noop", [P, TT]),
            "block_row": sb("block_row", [P, L0_BLOCKS], I32),
            "cleared": ctx.enter_context(nc.semaphore("cleared")),
        }
        constants_phase(nc, shared, dram)
        for layer in range(2):
            mine = {**dram, **{k[3:]: v for k, v in dram.items() if k.startswith(f"L{layer}_")}}
            attention_phase(nc, layer, shared, mine, layer == 0)
            with ExitStack() as experts:
                buffers = expert_buffers(nc, experts, layer)
                route_phase(nc, layer, shared, mine, buffers)
                expert_phase(nc, layer, shared, mine, buffers)
        combine_phase(nc, shared, dram)


def kernel(**inputs):
    import numpy as np
    import concourse.bacc as bacc
    from concourse import mybir as mb
    from concourse.bass_utils import run_bass_kernel_spmd

    nc = bacc.Bacc("TRN2", target_bir_lowering=False, num_devices=1)

    def rows(a):
        return np.broadcast_to(a.reshape(1, -1), (P, a.size))

    def heads_column(bias):
        a = bias.reshape(CH, HG, 1, HD)
        return np.broadcast_to(a, (CH, HG, 2, HD)).reshape(CH, P).T

    a = {"x": inputs["x"].reshape(N, D), "ctx_t": inputs["ctx_1024"].reshape(N, D).T,
         "gates": rows(np.concatenate([inputs["g_xattn"], inputs["g_ffn"]]))}
    for l in ("L0", "L1"):
        for n in "qkvo":
            a[f"{l}_w{n}"] = inputs[f"{l}_xattn_W{n}"].T
        for n in "qk":
            a[f"{l}_b{n}"] = heads_column(inputs[f"{l}_xattn_b{n}"])
        for n in "vo":
            a[f"{l}_b{n}"] = rows(inputs[f"{l}_xattn_b{n}"])
    b2 = np.broadcast_to(inputs["L0_ffn_b2"].reshape(E, 1, D), (E, P, D)).reshape(-1, D)
    a["L0_w1"] = np.concatenate([inputs["L0_ffn_W1"].reshape(-1, KC * F), inputs["L0_ffn_b1"].reshape(-1, FC)], axis=1)
    a["L0_w2"] = np.concatenate([inputs["L0_ffn_W2"].reshape(-1, FC * D), b2], axis=1)
    a["L1_w1"] = inputs["L1_ffn_experts_inter"].reshape(-1, KC * F)
    a["L1_w2"] = inputs["L1_ffn_experts_out"].reshape(-1, FC * D)
    a["L0_gate_w"] = inputs["L0_ffn_gate_w"]
    a["L1_gate_w"] = inputs["L1_ffn_router_w"].T
    a["L1_gate_b"] = rows(inputs["L1_ffn_router_b"])
    arrays = {k: np.ascontiguousarray(v) for k, v in a.items()}
    dram = {k: nc.dram_tensor(k, v.shape, mb.dt.from_np(v.dtype), kind="ExternalInput").ap() for k, v in arrays.items()}
    dram["xn"] = nc.dram_tensor("normalised", (N, D), F32, kind="Internal").ap()
    dram["ye"] = nc.dram_tensor("expert_out", (SLOTS + 1, D), F32, kind="Internal").ap()
    dram["out"] = nc.dram_tensor("out", (N, D), F32, kind="ExternalOutput").ap()
    program(nc, dram)
    result = run_bass_kernel_spmd(nc, [arrays], core_ids=[0])
    return result.results[0]["out"].reshape(B, S, D)
```
